# Optimizing a Trainium2 kernel written in Bass

```python
import numpy as np
import jax
import jax.numpy as jnp

def _softmax(x, axis=-1):
    return jax.nn.softmax(x, axis=axis)

def _gelu(x):
    return jax.nn.gelu(x, approximate=True)

def _silu(x):
    return jax.nn.silu(x)

def _sigmoid(x):
    return jax.nn.sigmoid(x)

def _layernorm(x, axis=-1, eps=1e-05):
    m = jnp.mean(x, axis=axis, keepdims=True)
    v = jnp.var(x, axis=axis, keepdims=True)
    return (x - m) / jnp.sqrt(v + eps)

def _scatter_add(tgt, idx, src, axis=0):
    return tgt.at[idx].add(src)

def _segment_sum(src, seg, n):
    return jax.ops.segment_sum(src, seg, n)
kernel_name = 'mk_flamingo_gated_d1_seqx_r8_630d84'

def setup_inputs(seed: int=0):
    np.random.seed(seed)
    _w = jnp.asarray

    def _rec_inputs():
        import jax
        import jax.numpy as jnp
        _rk = jax.random.key(seed)
        x = -0.000125 + 0.9999 * jax.random.normal(jax.random.fold_in(_rk, 1), (32, 64, 256), jnp.float32)
        _lenS = 64 - jax.random.randint(jax.random.fold_in(_rk, 7), (32,), 0, max(1, 64 // 4) + 1, jnp.int32)
        _lenS2 = 64 - jax.random.randint(jax.random.fold_in(_rk, 8), (32,), 0, max(1, 64 // 4) + 1, jnp.int32)
        _ctx_2048P = jax.random.normal(jax.random.fold_in(_rk, 11), (32, 16, 256), jnp.float32)
        _ctx_2048c = jax.random.dirichlet(jax.random.fold_in(_rk, 511), 0.3 * jnp.ones((16,), jnp.float32), (32, 64))
        _ctx_2048t = jnp.einsum('bsk,bkd->bsd', _ctx_2048c, _ctx_2048P)
        _ctx_2048t = _ctx_2048t * jax.lax.rsqrt(jnp.mean(jnp.square(_ctx_2048t)) + 1e-12) * 0.953939
        ctx_2048 = -0.000514642 + 1.00011 * (_ctx_2048t + 0.3 * jax.random.normal(jax.random.fold_in(_rk, 611), (32, 64, 256), jnp.float32))
        _validS = jnp.arange(64)[None, :] < _lenS[:, None]
        _validS2 = jnp.arange(64)[None, :] < _lenS2[:, None]
        _causal = jnp.tril(jnp.ones((64, 64), dtype=bool))
        mask_BxS2_bk0 = jnp.logical_not(jnp.broadcast_to(_validS2[:, :], (32, 64)))
        _g = jax.random.normal(jax.random.fold_in(_rk, 9001), (2, 1), jnp.float32)
        _g = jnp.sign(_g) * jnp.maximum(jnp.abs(_g), 1.0) + (_g == 0) * 1.0
        g_xattn = _g[0]
        g_ffn = _g[1]
        return (x, ctx_2048, mask_BxS2_bk0, g_xattn, g_ffn)
    x, ctx_2048, mask_BxS2_bk0, g_xattn, g_ffn = _rec_inputs()

    def _L0_xattn_setup():
        import jax, jax.numpy as jnp
        import numpy as np
        key = jax.random.key(seed)
        k1, k2, k3 = jax.random.split(key, 3)
        B, S, D, M = (8, 256, 256, 128)
        hidden_states = jax.random.normal(k1, (B, S, D), dtype=jnp.float32)
        memory_tokens = jax.random.normal(k2, (B, M, D), dtype=jnp.float32)
        memory_mask = jax.random.randint(k3, (B, M), 0, 2).astype(jnp.bool_)
        return {'hidden_states': hidden_states, 'memory_tokens': memory_tokens, 'memory_mask': memory_mask}
    _L0_xattn_all = _L0_xattn_setup()
    _L0_xattn_in = {k: v for k, v in _L0_xattn_all.items() if k in ()}
    del _L0_xattn_all

    def _L0_ffn_setup():
        import jax, jax.numpy as jnp
        import numpy as np
        H, I, E = (256, 512, 8)
        B, S = (2, 256)
        key = jax.random.key(seed)
        ks = jax.random.split(key, 5)
        scale = 0.02
        return {'hidden_states': jax.random.normal(ks[0], (B, S, H), dtype=jnp.float32), 'router_w': jax.random.normal(ks[1], (H, E), dtype=jnp.float32) * scale, 'gate_w': jax.random.normal(ks[2], (E, H, I), dtype=jnp.float32) * scale, 'up_w': jax.random.normal(ks[3], (E, H, I), dtype=jnp.float32) * scale, 'down_w': jax.random.normal(ks[4], (E, I, H), dtype=jnp.float32) * scale}
    _L0_ffn_all = _L0_ffn_setup()
    _L0_ffn_in = {k: v for k, v in _L0_ffn_all.items() if k in ('router_w', 'gate_w', 'up_w', 'down_w')}
    del _L0_ffn_all
    return {'x': x, 'ctx_2048': ctx_2048, 'mask_BxS2_bk0': mask_BxS2_bk0, 'g_xattn': g_xattn, 'g_ffn': g_ffn, 'L0_ffn_router_w': _L0_ffn_in['router_w'], 'L0_ffn_gate_w': _L0_ffn_in['gate_w'], 'L0_ffn_up_w': _L0_ffn_in['up_w'], 'L0_ffn_down_w': _L0_ffn_in['down_w']}

def reference(x, ctx_2048, mask_BxS2_bk0, g_xattn, g_ffn, L0_ffn_router_w, L0_ffn_gate_w, L0_ffn_up_w, L0_ffn_down_w):
    import jax
    import jax.numpy as jnp

    def _L0_xattn_ref(hidden_states, memory_tokens, memory_mask):
        import jax, jax.numpy as jnp
        import numpy as np
        B, S, D = hidden_states.shape
        scale = 1.0 / jnp.sqrt(jnp.asarray(D, hidden_states.dtype))
        scores = jnp.einsum('bsd,bmd->bsm', hidden_states, memory_tokens) * scale
        neg_inf = jnp.asarray(-1e+30, scores.dtype)
        scores = jnp.where(memory_mask[:, None, :], scores, neg_inf)
        attn = jax.nn.softmax(scores, axis=-1)
        readout = jnp.einsum('bsm,bmd->bsd', attn, memory_tokens)
        valid_b = jnp.any(memory_mask, axis=-1)
        out = jnp.where(valid_b[:, None, None], readout, jnp.zeros_like(readout))
        return out

    def _L0_ffn_ref(hidden_states, router_w, gate_w, up_w, down_w):
        import jax, jax.numpy as jnp
        import numpy as np
        H, I, E = (256, 512, 8)
        B, S = (2, 256)
        hidden_shape = hidden_states.shape
        x = hidden_states.reshape(-1, hidden_shape[-1])
        route = jax.nn.sigmoid(x @ router_w)
        max_ind = jnp.argmax(route, axis=1)
        max_prob = jnp.take_along_axis(route, max_ind[:, None], axis=1)
        out = jnp.zeros_like(x)
        num_experts = gate_w.shape[0]
        for e in range(num_experts):
            mask = (max_ind == e)[:, None]
            h = jax.nn.silu(x @ gate_w[e]) * (x @ up_w[e])
            out = out + jnp.where(mask, h @ down_w[e], 0.0)
        out = out * max_prob
        return out.reshape(hidden_shape)
    x = x + jnp.tanh(g_xattn[0]) * _L0_xattn_ref(_layernorm(x, axis=-1), ctx_2048, mask_BxS2_bk0)
    x = x + jnp.tanh(g_ffn[0]) * _L0_ffn_ref(_layernorm(x, axis=-1), L0_ffn_router_w, L0_ffn_gate_w, L0_ffn_up_w, L0_ffn_down_w)
    return x

_drawn_inputs = setup_inputs


def setup_inputs(seed=0):
    import zlib

    import numpy as np

    out = dict(_drawn_inputs(seed))
    spreads = {}
    factors = {'L0_ffn_router_w': 5.008,
     'L0_ffn_gate_w': 4.719,
     'L0_ffn_up_w': 4.668,
     'L0_ffn_down_w': 4.667}
    for name, (base, spread) in spreads.items():
        noise = np.random.default_rng([zlib.crc32(name.encode()), seed]).standard_normal(out[name].shape)
        drawn = base * np.exp(spread * noise) if base else spread * noise
        out[name] = jnp.asarray(drawn.astype(out[name].dtype))
    for name, factor in factors.items():
        out[name] = (out[name] * factor).astype(out[name].dtype)
    return out
```

```python
from contextlib import ExitStack

import concourse.bass as bass
from concourse import mybir
from concourse.alu_op_type import AluOpType as ALU

F32 = mybir.dt.float32
F32R = mybir.dt.float32r
BF16 = mybir.dt.bfloat16
F16 = mybir.dt.float16
I32 = mybir.dt.int32
U8 = mybir.dt.uint8
ACT = mybir.ActivationFunctionType
AX = mybir.AxisListType

P = 128
NEG = -1e30
EPS = 1e-5


class Steps:

    def __init__(self, engine, sem):
        self.engine, self.sem, self.base, self.n = engine, sem, 0, 0

    def done(self, instruction, apart=None):
        instruction.then_inc(self.sem, 1)
        self.n += 1
        if apart:
            return apart(self.engine, (self.sem, self.base + self.n))
        self.engine.wait_ge(self.sem, self.base + self.n)

    def enter(self, i, per_turn):
        self.start, self.base, self.n = self.base + self.n, self.base + self.n + i * per_turn, 0

    def leave(self, turns, per_turn):
        assert self.n == per_turn, (self.n, per_turn)
        self.base, self.n = self.start + turns * per_turn, 0


def apart_after(met):
    def apart(engine, *waits):
        waits = [(s, v if isinstance(v, int) else engine.to_reg(v)) for s, v in waits]
        engine.wait_ge(met, 1)
        for s, v in waits:
            wait(engine, s, v)
    return apart


class At:

    def __init__(self, i, of, c):
        self.i, self.of, self.c = i, of, c

    def __add__(self, d):
        return At(self.i, self.of, self.c + d)

    def __sub__(self, d):
        return At(self.i, self.of, self.c - d)

    @property
    def n(self):
        return self.c if self.i is None else self.i * self.of + self.c

    def slot(self, ring):
        return self.c % ring

    def use(self, ring):
        return self.c // ring if self.i is None else self.i * (self.of // ring) + self.c // ring


def wait(engine, sem, value):
    if not isinstance(value, int) or value > 0:
        engine.wait_ge(sem, value)


def gated_block(nc, x, ctx, mask, g_xattn, g_ffn, router_w, gate_w, up_w, down_w, out):
    B, S, D = x.shape
    E, _, I = gate_w.shape
    TOK = B * S
    T = TOK // P
    PAIRS = T // 2
    KD, KI = D // P, I // P
    SLOTS = (TOK - E) // P + E
    SL = SLOTS + 1
    COLS = D + 4
    WM = KD * I
    WDN = KI * D
    SCALE = 1.0 / float(D) ** 0.5

    x_v = x.rearrange("b s d -> (b s) d").rearrange("(t p) d -> p t d", p=P)
    ctx_v = ctx.rearrange("b s d -> (b s) d").rearrange("(t p) d -> p t d", p=P)
    out_v = out.rearrange("b s d -> (b s) d")
    mask_v = mask.rearrange("(t b) m -> b t m", b=2)
    table = nc.dram_tensor("rows_by_token", [TOK, COLS], F32).ap()
    table_v = table.rearrange("(t p) c -> p t c", p=P)

    def gate_up(w, e):
        return w[bass.ds(e, 1), :, :].rearrange("a (k p) n -> p (a k) n", p=P)

    with ExitStack() as stack:
        def sb(name, shape, dt=F32, on=stack):
            return on.enter_context(nc.sbuf_tensor(name, shape, dt))

        def pb(name, on, shape=(P, 512)):
            return on.enter_context(nc.psum_tensor(name, list(shape), F32))

        def sem(name):
            return stack.enter_context(nc.semaphore(name))

        w_hi = sb("w_hi", [P, E * 2 * WM], F32R)
        w_lo = sb("w_lo", [P, E * 2 * WM], F32R)
        w_dn = sb("w_dn", [P, E * WDN])
        ident = sb("ident", [P, P])
        slot_idx = sb("slot_idx", [P, SL], I32)
        slot_now = sb("slot_now", [P, 4], I32)
        tile_expert = sb("tile_expert", [1, SL], I32)

        stage = sb("stage", [P, 2, 2, WM])
        router = sb("router", [P, KD, E])
        bias = sb("bias", [2, T, P], BF16)
        any2 = sb("any2", [2, T], BF16)
        batch_of = sb("batch_of", [2, P], BF16)
        ones_b = sb("ones_b", [P, P], BF16)
        tri_b = sb("tri_b", [P, P], BF16)
        onehot = sb("onehot", [P, E, T], BF16)
        gates = sb("gates", [P, 2])
        tanhs = sb("tanhs", [P, 2])
        coef_x = sb("coef_x", [P, T])
        minus_half = sb("minus_half", [P, 2])
        ones8 = sb("ones8", [P, E])
        rev8 = sb("rev8", [P, E])
        bn1 = sb("bn1", [P, 2, 6])
        mv1 = sb("mv1", [P, 2, 2])
        ve1 = sb("ve1", [P, 2])
        rs1 = sb("rs1", [P, 2])
        nb1 = sb("nb1", [P, 2])
        bn2 = sb("bn2", [P, 2, 6])
        mv2 = sb("mv2", [P, 2, 2])
        ve2 = sb("ve2", [P, 2])
        rmax = sb("rmax", [P, 2])
        nmax = sb("nmax", [P, 2])
        rsum = sb("rsum", [P, 2])
        rinv = sb("rinv", [P, 2])
        cs = sb("cs", [P, 2])
        ez = sb("ez", [P, 2, E])
        route = sb("route", [P, 2, E])
        best = sb("best", [P, 2])
        key = sb("key", [P, 2])

        one = ExitStack()
        a = lambda name, shape, dt=F32: sb(name, shape, dt, one)
        x_sb = a("x_sb", [P, 2, 2, D])
        ctx_sb = a("ctx_sb", [P, 2, 2, D])
        row = a("row", [P, 2, 2, COLS])
        xn = a("xn", [P, 2, D])
        xnT = a("xnT", [P, KD, 2 * P])
        ctxT = a("ctxT", [P, KD, 2 * P])
        probs = a("probs", [P, 2, P])
        probsT = a("probsT", [P, 2, P])
        x2n = a("x2n", [P, 2, D])
        x2nT = a("x2nT", [P, KD, 2 * P])
        logits = a("logits", [E, 2 * P])
        mask2 = x2nT[0:2, :, :].rearrange("b k t -> b (k t)").bitcast(U8).rearrange("b (t m) -> b t m", t=T)
        ps_x = pb("ps_x", one, (P, KD, 2 * P))
        ps_c = pb("ps_c", one, (P, KD, 2 * P))
        ps_s = pb("ps_s", one)
        ps_p = pb("ps_p", one)
        ps_r = pb("ps_r", one, (P, 2, D))
        ps_x2 = pb("ps_x2", one, (P, KD, 2 * P))
        ps_l = pb("ps_l", one)
        ps_b = pb("ps_b", one)
        one.close()

        xg = sb("xg", [P, 4, COLS])
        fx = sb("fx", [P, D])
        fxT_hi = sb("fxT_hi", [P, KD, P], F32R)
        fxT_lo = sb("fxT_lo", [P, KD, P], F32R)
        sil = sb("sil", [P, I])
        h = sb("h", [P, I])
        hT = sb("hT", [P, KI, P])
        yo = sb("yo", [P, 2, D])
        thr = sb("thr", [P, T])
        iota_sl = sb("iota_sl", [P, SL])
        iota_p = sb("iota_p", [P, P], F16)
        tok_m = sb("tok_m", [P, T])
        count_sb = sb("count_sb", [P, E, T])
        upto = sb("upto", [P, E, T])
        rank = sb("rank", [P, E, T])
        keep = sb("keep", [P, E, T])
        over = sb("over", [P, E, T])
        ntile = sb("ntile", [P, E])
        tend = sb("tend", [P, E])
        tstart = sb("tstart", [P, E])
        pos = sb("pos", [P, T])
        pos_i = sb("pos_i", [P, T], I32)
        pos_a = sb("pos_a", [P, T], I32)
        pos_b = sb("pos_b", [P, T], I32)
        a_hot = sb("a_hot", [P, T, SL], F16)
        a_val = sb("a_val", [P, T, SL], F16)
        b_hot = sb("b_hot", [P, T, P], F16)
        past = sb("past", [1, SL, E])
        past_n = sb("past_n", [1, SL])
        pf_g = pb("pf_g", stack)
        pf_u = pb("pf_u", stack)
        pf_x = pb("pf_x", stack, (P, KD, P))
        pf_h = pb("pf_h", stack, (P, KI, P))
        pf_y = pb("pf_y", stack)

        x_in = [sem(f"x_in{s}") for s in range(2)]
        ctx_in = [sem(f"ctx_in{s}") for s in range(2)]
        small_in = sem("small_in")
        mask_in = sem("mask_in")
        gate_in = [sem(f"gate_in{s}") for s in range(2)]
        up_in = [sem(f"up_in{s}") for s in range(2)]
        down_in = sem("down_in")
        row_out = [sem(f"row_out{s}") for s in range(2)]
        gathered = [sem(f"gathered{s}") for s in range(4)]
        stored = [sem(f"stored{s}") for s in range(2)]
        mask_clear = sem("mask_clear")
        keep_ready = sem("keep_ready")
        const_ready = sem("const_ready")
        bias_ready = sem("bias_ready")
        tanh_ready = sem("tanh_ready")
        valid_ready = sem("valid_ready")
        (scores_ready, negmax_ready, exp_done, pT_done, pT_ready, readout_done, x2_done,
         var1_ready, rstd1_ready, xn_ready, xT_done, xnT_ready, cT_done, ctxT_ready,
         var2_ready, rstd2_ready, x2n_ready, x2T_done, x2nT_ready, logits_done, lg_ready,
         lb_done, expz_done, route_ready, whi_ready, wlo_ready) = [sem(n) for n in (
            "scores_ready", "negmax_ready", "exp_done", "pT_done", "pT_ready", "readout_done",
            "x2_done", "var1_ready", "rstd1_ready", "xn_ready", "xT_done", "xnT_ready", "cT_done",
            "ctxT_ready", "var2_ready", "rstd2_ready", "x2n_ready", "x2T_done", "x2nT_ready",
            "logits_done", "lg_ready", "lb_done", "expz_done", "route_ready", "whi_ready",
            "wlo_ready")]
        counts_done, ahot_ready, aval_ready, b_ready, slots_done, idx_ready, expert_ready, xg_clear = [
            sem(n) for n in ("counts_done", "ahot_ready", "aval_ready", "b_ready", "slots_done",
                             "idx_ready", "expert_ready", "xg_clear")]
        (g_done, u_done, silu_done, h_ready, hT_done, hT_ready, down_done, y_ready, fx_ready,
         fxT_done, xhi_ready, xlo_ready, idx_copied) = [sem(n) for n in (
            "g_done", "u_done", "silu_done", "h_ready", "hT_done", "hT_ready", "down_done",
            "y_ready", "fx_ready", "fxT_done", "xhi_ready", "xlo_ready", "idx_copied")]
        dve_steps, act_steps, pool_steps = sem("dve_steps"), sem("act_steps"), sem("pool_steps")

        apart = apart_after(const_ready)
        block = stack.enter_context(nc.Block())

        PEEL, TURNS = 2, (PAIRS - 2) // 2
        FTURNS = (SLOTS - 3) // 4

        def pairs(engine, body, steps=None, per_turn=0):
            for k in range(PEEL):
                body(At(None, 0, k))
            with engine.Fori(0, TURNS) as i:
                if steps:
                    steps.enter(i, per_turn)
                for u in range(2):
                    body(At(i, 2, PEEL + u))
            if steps:
                steps.leave(TURNS, per_turn)
            for k in range(PAIRS, PAIRS + 2):
                body(At(None, 0, k))

        def enters(k):
            return k.i is not None or k.c < PAIRS

        def second(k):
            return k.i is not None or 1 <= k.c <= PAIRS

        def third(k):
            return k.i is not None or k.c >= 2

        def tiles(engine, body):
            body(At(None, 0, 0))
            with engine.Fori(0, FTURNS) as i:
                for u in range(4):
                    body(At(i, 4, 1 + u))
            for j in range(1 + 4 * FTURNS, SLOTS):
                body(At(None, 0, j))

        def last(j):
            return j.i is None and j.c == SLOTS - 1

        @block.sync
        def _(sp):
            def load_pair(k):
                wait(sp, x2_done, (k - 1).n)
                wait(sp, readout_done, (k - 1).n)
                sp.dma_start(x_sb[:, k.slot(2), :, :], x_v[:, bass.ds(k.n * 2, 2), :]).then_inc(x_in[k.slot(2)], 16)
                sp.dma_start(ctx_sb[:, k.slot(2), :, :], ctx_v[:, bass.ds(k.n * 2, 2), :]).then_inc(ctx_in[k.slot(2)], 16)

            def load_expert(k):
                wait(sp, wlo_ready, 2 * (k - 1).n)
                s = stage[:, k.slot(2), :, :].rearrange("p m (k n) -> p m k n", k=KD)
                sp.dma_start(s[:, 0, :, :], gate_up(gate_w, k.n)).then_inc(gate_in[k.slot(2)], 16)
                sp.dma_start(s[:, 1, :, :], gate_up(up_w, k.n)).then_inc(up_in[k.slot(2)], 16)

            def store_rows(k):
                sp.wait_ge(route_ready, (k + 1).n)
                sp.dma_start(table_v[:, bass.ds(k.n * 2, 2), :], row[:, k.slot(2), :, :]).then_inc(row_out[k.slot(2)], 16)

            first = At(None, 0, 0)
            load_pair(first)
            for b in range(2):
                sp.wait_ge(mask_clear, 1)
                sp.dma_start(mask2[b:b + 1, :, b * S:(b + 1) * S], mask_v[b:b + 1, :, :]).then_inc(mask_in, 16)
            sp.dma_start(gates[:, 0:1], g_xattn.partition_broadcast(P)).then_inc(small_in, 16)
            sp.dma_start(gates[:, 1:2], g_ffn.partition_broadcast(P)).then_inc(small_in, 16)
            sp.dma_start(router[:, :, :], router_w.rearrange("(k p) e -> p k e", p=P)).then_inc(small_in, 16)
            load_expert(first)

            def turn(k):
                if k.i is not None or k.c < PAIRS - 1:
                    load_pair(k + 1)
                    load_expert(k + 1)
                if third(k):
                    store_rows(k - 2)

            for c in range(PEEL):
                turn(At(None, 0, c))
            with sp.Fori(0, TURNS - 1) as i:
                for u in range(2):
                    turn(At(i, 2, PEEL + u))
            for c in range(PAIRS - 2, PAIRS + 2):
                turn(At(None, 0, c))
            for e in range(E):
                sp.dma_start(w_dn[:, e * WDN:(e + 1) * WDN].rearrange("p (k n) -> p k n", k=KI),
                             down_w[e, :, :].rearrange("(k p) n -> p k n", p=P)).then_inc(down_in, 16)

        @block.gpsimd
        def _(pool):
            steps = Steps(pool, pool_steps)
            pool.memset(mask2[:, :, :], 0).then_inc(mask_clear, 1)
            pool.memset(ident[:, :], 0.0)
            pool.memset(ones_b[:, :], 1.0)
            pool.memset(tri_b[:, :], 1.0)
            pool.memset(batch_of[:, :], 1.0)
            pool.memset(minus_half[:, :], -0.5)
            steps.done(pool.memset(ones8[:, :], 1.0))
            pool.affine_select(out=ident[:, :], in_=ident[:, :], compare_op=ALU.not_equal, fill=1.0,
                               base=0, pattern=[[-1, P]], channel_multiplier=1)
            pool.affine_select(out=tri_b[:, :], in_=tri_b[:, :], compare_op=ALU.is_gt, fill=0.0,
                               base=0, pattern=[[1, P]], channel_multiplier=-1)
            steps.done(pool.affine_select(out=batch_of[:, :], in_=batch_of[:, :], compare_op=ALU.is_ge, fill=0.0,
                                          base=0, pattern=[[1, P]], channel_multiplier=-S))
            pool.affine_select(out=batch_of[:, :], in_=batch_of[:, :], compare_op=ALU.is_ge, fill=0.0,
                               base=S - 1, pattern=[[-1, P]], channel_multiplier=S)
            loose = dict(allow_small_or_imprecise_dtypes=True)
            pool.iota(rev8[:, :], [[-1, E]], base=E, channel_multiplier=0, **loose).then_inc(const_ready, 1)

            def split_lo(k, m):
                apart(pool, (whi_ready, 2 * k.n + m + 1))
                at = bass.ds(k.n * (2 * WM) + m * WM, WM)
                pool.tensor_tensor(w_lo[:, at], stage[:, k.slot(2), m, :], w_hi[:, at].bitcast(F32),
                                   ALU.subtract).then_inc(wlo_ready, 1)

            pool.wait_ge(const_ready, 1)

            def turn(k):
                if enters(k):
                    pool.wait_ge(var1_ready, (k + 1).n)
                    wait(pool, xn_ready, k.n)
                    pool.tensor_tensor(rs1[:, :], ve1[:, :], minus_half[:, :], ALU.pow).then_inc(rstd1_ready, 1)
                    split_lo(k, 0)
                if second(k):
                    pool.wait_ge(var2_ready, k.n)
                    pool.tensor_tensor(row[:, (k - 1).slot(2), :, D], ve2[:, :], minus_half[:, :],
                                       ALU.pow).then_inc(rstd2_ready, 1)
                if enters(k):
                    split_lo(k, 1)

            pairs(pool, turn)
            pool.wait_ge(route_ready, PAIRS)
            steps.done(pool.memset(keep[:, :, :], 1.0))
            pool.iota(thr[:, :], [[P, T]], base=0, channel_multiplier=0, **loose)
            pool.iota(iota_sl[:, :], [[1, SL]], base=0, channel_multiplier=0, **loose)
            pool.iota(iota_p[:, :], [[1, P]], base=0, channel_multiplier=0, **loose)
            pool.iota(tok_m[:, :], [[P, T]], base=-TOK, channel_multiplier=1, **loose)
            pool.affine_select(out=keep[:, :, :], in_=keep[:, :, :], compare_op=ALU.not_equal, fill=0.0,
                               base=0, pattern=[[0, E], [1, T]], channel_multiplier=0).then_inc(keep_ready, 1)
            pool.wait_ge(ahot_ready, 1)
            pool.tensor_tensor(a_val[:, :, :], a_hot[:, :, :],
                               tok_m[:, :].unsqueeze(2).to_broadcast([P, T, SL]), ALU.mult).then_inc(aval_ready, 1)

            def gather(j):
                apart(pool, (y_ready, (j - 3).n))
                pool.tensor_copy(slot_now[:, j.slot(4):j.slot(4) + 1], slot_idx[:, bass.ds(j.n, 1)]).then_inc(idx_copied, 1)
                apart(pool, (idx_copied, (j + 1).n))
                pool.indirect_dma_start(
                    xg[:, j.slot(4), :], None, table,
                    bass.IndirectOffsetOnAxis(ap=slot_now[:, j.slot(4):j.slot(4) + 1], axis=0),
                    bounds_check=TOK - 1, oob_is_err=False).then_inc(gathered[j.slot(4)], 16)

            def scatter(j):
                apart(pool, (y_ready, (j + 1).n))
                pool.indirect_dma_start(
                    out_v, bass.IndirectOffsetOnAxis(ap=slot_now[:, j.slot(4):j.slot(4) + 1], axis=0),
                    yo[:, j.slot(2), :], None,
                    bounds_check=TOK - 1, oob_is_err=False).then_inc(stored[j.slot(2)], 16)

            for s in range(2):
                pool.wait_ge(row_out[s], 16 * (PAIRS // 2))
            pool.wait_ge(xg_clear, 1)
            pool.wait_ge(idx_ready, 1)
            for c in range(3):
                gather(At(None, 0, c))

            def turn_f(j):
                if j.i is not None or j.c > 0:
                    scatter(j - 1)
                if j.i is not None or j.c + 3 < SLOTS:
                    if j.i is not None or j.c > 0:
                        pool.wait_ge(stored[(j - 1).slot(2)], 16 * ((j - 1).use(2) + 1))
                    gather(j + 3)

            turn_f(At(None, 0, 0))
            turns = (SLOTS - 4) // 4
            with pool.Fori(0, turns) as i:
                for u in range(4):
                    turn_f(At(i, 4, 1 + u))
            for j in range(1 + 4 * turns, SLOTS):
                turn_f(At(None, 0, j))
            scatter(At(None, 0, SLOTS - 1))
            for s in range(2):
                pool.wait_ge(stored[s], 16 * ((SLOTS + 1 - s) // 2))

        @block.scalar
        def _(act):
            act.wait_ge(small_in, 48)
            act.activation(tanhs[:, :], gates[:, :], ACT.Tanh).then_inc(tanh_ready, 1)

            def split_hi(k, m):
                act.wait_ge((gate_in, up_in)[m][k.slot(2)], 16 * (k.use(2) + 1))
                at = bass.ds(k.n * (2 * WM) + m * WM, WM)
                act.activation(w_hi[:, at], stage[:, k.slot(2), m, :], ACT.Copy).then_inc(whi_ready, 1)

            def turn(k):
                n, m = k - 1, k - 2
                if second(k):
                    act.wait_ge(negmax_ready, (n + 1).n)
                    wait(act, pT_done, n.n)
                    for t in range(2):
                        e = act.activation(probs[:, t, :], ps_s[:, t * P:(t + 1) * P], ACT.Exp, bias=nmax[:, t:t + 1],
                                           scale=SCALE, accum_out=rsum[:, t:t + 1])
                    e.then_inc(exp_done, 1)
                if third(k):
                    act.wait_ge(x2T_done, (m + 1).n)
                    wait(act, logits_done, m.n)
                    act.activation(x2nT[:, :, :], ps_x2[:, :, :], ACT.Copy).then_inc(x2nT_ready, 1)
                if enters(k):
                    act.wait_ge(cT_done, (k + 1).n)
                    wait(act, scores_ready, k.n)
                    act.activation(ctxT[:, :, :], ps_c[:, :, :], ACT.Copy).then_inc(ctxT_ready, 1)
                if second(k):
                    act.wait_ge(pT_done, (n + 1).n)
                    wait(act, readout_done, n.n)
                    act.activation(probsT[:, :, :], ps_p[:, 0:2 * P].rearrange("p (t m) -> p t m", t=2),
                                   ACT.Copy).then_inc(pT_ready, 1)
                if enters(k):
                    split_hi(k, 0)
                if third(k):
                    act.wait_ge(logits_done, (m + 1).n)
                    wait(act, lb_done, m.n)
                    act.activation(logits[:, :], ps_l[0:E, 0:2 * P], ACT.Copy).then_inc(lg_ready, 1)
                if enters(k):
                    act.wait_ge(xT_done, (k + 1).n)
                    act.activation(xnT[:, :, :], ps_x[:, :, :], ACT.Copy).then_inc(xnT_ready, 1)
                    split_hi(k, 1)
                if third(k):
                    act.wait_ge(lb_done, (m + 1).n)
                    wait(act, route_ready, m.n)
                    act.activation(ez[:, :, :], ps_b[:, 0:2 * E].rearrange("p (t e) -> p t e", t=2), ACT.Exp,
                                   scale=-1.0).then_inc(expz_done, 1)

            pairs(act, turn)

            def x_hi(j):
                act.wait_ge(fxT_done, (j + 1).n)
                wait(act, u_done, j.n)
                wait(act, xlo_ready, j.n)
                act.activation(fxT_hi[:, :, :], pf_x[:, :, :], ACT.Copy).then_inc(xhi_ready, 1)

            x_hi(At(None, 0, 0))

            def tile(j):
                act.wait_ge(g_done, (j + 1).n)
                wait(act, h_ready, j.n)
                act.activation(sil[:, :], pf_g[:, :], ACT.Silu).then_inc(silu_done, 1)
                if not last(j):
                    x_hi(j + 1)
                act.wait_ge(hT_done, (j + 1).n)
                wait(act, down_done, j.n)
                act.activation(hT[:, :, :], pf_h[:, :, :], ACT.Copy).then_inc(hT_ready, 1)

            tiles(act, tile)

        @block.vector
        def _(dve):
            steps = Steps(dve, dve_steps)
            done = steps.done
            dve.wait_ge(mask_in, 32)
            dve.tensor_scalar(bias[:, :, :], mask2[:, :, :], 1.0, -NEG, ALU.subtract, ALU.mult)
            dve.tensor_reduce(any2[:, :], mask2[:, :, :], axis=AX.X, op=ALU.max).then_inc(bias_ready, 1)

            def ln_stats(rows, bn, mv, ve, ready):
                for t in range(2):
                    i = dve.bn_stats(bn[:, t, :], rows[:, t, 0:D])
                done(i, apart)
                for t in range(2):
                    i = dve.bn_aggr(mv[:, t, :], bn[:, t, :])
                done(i)
                dve.tensor_scalar(ve[:, :], mv[:, :, 1], EPS, None, ALU.add).then_inc(ready, 1)

            def turn(k):
                n, m = k - 1, k - 2
                if second(k):
                    dve.wait_ge(scores_ready, (n + 1).n)
                    done(dve.tensor_reduce(rmax[:, :], ps_s[:, 0:2 * P].rearrange("p (t m) -> p t m", t=2),
                                           axis=AX.X, op=ALU.max))
                    dve.tensor_scalar(nmax[:, :], rmax[:, :], -SCALE, None, ALU.mult).then_inc(negmax_ready, 1)
                if third(k):
                    r = row[:, m.slot(2), :, :]
                    dve.wait_ge(rstd2_ready, (m + 1).n)
                    wait(dve, x2T_done, m.n)
                    done(dve.scalar_tensor_tensor(r[:, :, D + 1], mv2[:, :, 0], -1.0, r[:, :, D], ALU.mult, ALU.mult))
                    for t in range(2):
                        i = dve.tensor_scalar(x2n[:, t, :], r[:, t, 0:D], r[:, t, D:D + 1], r[:, t, D + 1:D + 2],
                                              ALU.mult, ALU.add)
                    i.then_inc(x2n_ready, 1)
                if enters(k):
                    dve.wait_ge(x_in[k.slot(2)], 16 * (k.use(2) + 1))
                    ln_stats(x_sb[:, k.slot(2), :, :], bn1, mv1, ve1, var1_ready)
                if second(k):
                    dve.wait_ge(exp_done, (n + 1).n)
                    done(dve.reciprocal(rinv[:, :], rsum[:, :]))
                    done(dve.tensor_tensor(cs[:, :], rinv[:, :], coef_x[:, bass.ds(n.n * 2, 2)], ALU.mult))
                if enters(k):
                    dve.wait_ge(rstd1_ready, (k + 1).n)
                    wait(dve, xT_done, k.n)
                    done(dve.scalar_tensor_tensor(nb1[:, :], mv1[:, :, 0], -1.0, rs1[:, :], ALU.mult, ALU.mult))
                    for t in range(2):
                        i = dve.tensor_scalar(xn[:, t, :], x_sb[:, k.slot(2), t, :], rs1[:, t:t + 1], nb1[:, t:t + 1],
                                              ALU.mult, ALU.add)
                    i.then_inc(xn_ready, 1)
                if second(k):
                    dve.wait_ge(readout_done, (n + 1).n)
                    wait(dve, row_out[n.slot(2)], 16 * n.use(2))
                    for t in range(2):
                        i = dve.scalar_tensor_tensor(row[:, n.slot(2), t, 0:D], ps_r[:, t, :], cs[:, t:t + 1],
                                                     x_sb[:, n.slot(2), t, :], ALU.mult, ALU.add)
                    i.then_inc(x2_done, 1)
                    dve.wait_ge(x2_done, (n + 1).n)
                    ln_stats(row[:, n.slot(2), :, :], bn2, mv2, ve2, var2_ready)
                if third(k):
                    dve.wait_ge(expz_done, (m + 1).n)
                    done(dve.tensor_scalar(route[:, :, :], ez[:, :, :], 1.0, None, ALU.add))
                    done(dve.reciprocal(route[:, :, :], route[:, :, :]))
                    done(dve.tensor_reduce(best[:, :], route[:, :, :], axis=AX.X, op=ALU.max))
                    dve.tensor_scalar(row[:, m.slot(2), :, D + 2], best[:, :], tanhs[:, 1:2], None, ALU.mult)
                    done(dve.tensor_tensor(route[:, :, :], route[:, :, :],
                                           best[:, :].unsqueeze(2).to_broadcast([P, 2, E]), ALU.is_equal))
                    done(dve.tensor_tensor(route[:, :, :], route[:, :, :],
                                           rev8[:, :].unsqueeze(1).to_broadcast([P, 2, E]), ALU.mult))
                    done(dve.tensor_reduce(key[:, :], route[:, :, :], axis=AX.X, op=ALU.max))
                    dve.tensor_tensor(onehot[:, :, bass.ds(m.n * 2, 2)].rearrange("p e t -> p t e"),
                                      rev8[:, :].unsqueeze(1).to_broadcast([P, 2, E]),
                                      key[:, :].unsqueeze(2).to_broadcast([P, 2, E]),
                                      ALU.is_equal).then_inc(route_ready, 1)

            done(dve.memset(row[:, :, :, D + 3], 0.0))
            dve.wait_ge(valid_ready, 1)
            dve.wait_ge(tanh_ready, 1)
            dve.wait_ge(const_ready, 1)
            done(dve.tensor_scalar(coef_x[:, :], ps_b[:, 0:T], tanhs[:, 0:1], None, ALU.mult))
            pairs(dve, turn, steps, 2 * (1 + 1 + 2 + 2 + 1 + 2 + 6))

            dve.wait_ge(counts_done, 1)
            dve.wait_ge(keep_ready, 1)
            done(dve.tensor_copy(count_sb[:, :, :].rearrange("p e t -> p (e t)"), ps_x[:, 0, 0:E * T]))
            flat = lambda z: z[:, :, :].rearrange("p e t -> p (e t)")
            done(dve.tensor_tensor_scan(flat(upto), flat(keep), flat(count_sb), 0.0, ALU.mult, ALU.add))
            done(dve.tensor_tensor(over[:, :, :], upto[:, :, T - 1:T].to_broadcast([P, E, T]),
                                   thr[:, :].unsqueeze(1).to_broadcast([P, E, T]), ALU.is_gt))
            dve.tensor_tensor(rank[:, :, :], upto[:, :, :], count_sb[:, :, :], ALU.subtract)
            done(dve.tensor_reduce(ntile[:, :], over[:, :, :], axis=AX.X, op=ALU.add))
            done(dve.tensor_tensor_scan(tend[:, :], ones8[:, :], ntile[:, :], 0.0, ALU.mult, ALU.add))
            dve.tensor_tensor(tstart[:, :], tend[:, :], ntile[:, :], ALU.subtract)
            done(dve.tensor_tensor(flat(rank), flat(rank), ps_c[:, 0, 0:E * T], ALU.add))
            done(dve.scalar_tensor_tensor(rank[:, :, :], tstart[:, :].unsqueeze(2).to_broadcast([P, E, T]), float(P),
                                          rank[:, :, :], ALU.mult, ALU.add))
            done(dve.tensor_tensor(rank[:, :, :], rank[:, :, :], onehot[:, :, :], ALU.mult))
            done(dve.tensor_reduce(pos[:, :], rank[:, :, :].rearrange("p e t -> p t e"), axis=AX.X, op=ALU.add))
            done(dve.tensor_copy(pos_i[:, :], pos[:, :]))
            shift = P.bit_length() - 1
            dve.tensor_scalar(pos_a[:, :], pos_i[:, :], shift, None, ALU.logical_shift_right)
            done(dve.tensor_scalar(pos_b[:, :], pos_i[:, :], P - 1, None, ALU.bitwise_and))
            dve.tensor_tensor(a_hot[:, :, :], iota_sl[:, :].unsqueeze(1).to_broadcast([P, T, SL]),
                              pos_a[:, :].unsqueeze(2).to_broadcast([P, T, SL]), ALU.is_equal).then_inc(ahot_ready, 1)
            for q in range(4):
                t0, t1 = q * T // 4, (q + 1) * T // 4
                dve.tensor_tensor(b_hot[:, t0:t1, :], iota_p[:, :].unsqueeze(1).to_broadcast([P, t1 - t0, P]),
                                  pos_b[:, t0:t1].unsqueeze(2).to_broadcast([P, t1 - t0, P]),
                                  ALU.is_equal).then_inc(b_ready, 1)
            done(dve.tensor_tensor(past[:, :, :], iota_sl[0:1, :].unsqueeze(2).to_broadcast([1, SL, E]),
                                   tend[0:1, :].unsqueeze(1).to_broadcast([1, SL, E]), ALU.is_ge))
            done(dve.tensor_reduce(past_n[:, :], past[:, :, :], axis=AX.X, op=ALU.add))
            dve.tensor_scalar(tile_expert[:, :], past_n[:, :], float(E - 1), None, ALU.min).then_inc(expert_ready, 1)
            dve.wait_ge(slots_done, 1)
            dve.tensor_scalar(slot_idx[:, :], ps_s[:, 0:SL], float(TOK), None, ALU.add).then_inc(idx_ready, 1)
            dve.wait_ge(aval_ready, 1)
            for s in range(2):
                dve.wait_ge(row_out[s], 16 * (PAIRS // 2))
            dve.wait_ge(wlo_ready, 2 * E)
            dve.memset(xg[:, :, :], 0.0).then_inc(xg_clear, 1)

            def normalised(j):
                dve.wait_ge(gathered[j.slot(4)], 16 * (j.use(4) + 1))
                wait(dve, fxT_done, j.n)
                r = xg[:, j.slot(4), :]
                dve.tensor_scalar(fx[:, :], r[:, 0:D], r[:, D:D + 1], r[:, D + 1:D + 2],
                                  ALU.mult, ALU.add).then_inc(fx_ready, 1)

            def x_lo(j):
                dve.wait_ge(xhi_ready, (j + 1).n)
                wait(dve, u_done, j.n)
                dve.tensor_tensor(fxT_lo[:, :, :], pf_x[:, :, :], fxT_hi[:, :, :].bitcast(F32),
                                  ALU.subtract).then_inc(xlo_ready, 1)

            def output(j):
                dve.wait_ge(down_done, (j + 1).n)
                wait(dve, stored[j.slot(2)], 16 * j.use(2))
                r = xg[:, j.slot(4), :]
                dve.scalar_tensor_tensor(yo[:, j.slot(2), :], pf_y[:, 0:D], r[:, D + 2:D + 3], r[:, 0:D],
                                         ALU.mult, ALU.add).then_inc(y_ready, 1)

            first = At(None, 0, 0)
            normalised(first)
            x_lo(first)
            normalised(first + 1)

            def tile(j):
                dve.wait_ge(silu_done, (j + 1).n)
                dve.wait_ge(u_done, (j + 1).n)
                wait(dve, hT_done, j.n)
                dve.tensor_tensor(h[:, :], sil[:, :], pf_u[:, :], ALU.mult).then_inc(h_ready, 1)
                if not last(j):
                    x_lo(j + 1)
                    if not last(j + 1):
                        normalised(j + 2)
                if j.i is not None or j.c > 0:
                    output(j - 1)

            tiles(dve, tile)
            output(At(None, 0, SLOTS - 1))

        @block.tensor
        def _(pe):
            pe.wait_ge(const_ready, 1)
            pe.wait_ge(bias_ready, 1)
            pe.matmul(ps_b[:, 0:T], batch_of[:, :], any2[:, :], start=True, stop=True).then_inc(valid_ready, 1)

            def transposes(dst, src):
                for t in range(2):
                    for k in range(KD):
                        i = pe.transpose(dst[:, k, t * P:(t + 1) * P], src[:, t, k * P:(k + 1) * P], ident[:, :])
                return i

            def turn(k):
                n, m = k - 1, k - 2
                if second(k):
                    pe.wait_ge(xnT_ready, (n + 1).n)
                    pe.wait_ge(ctxT_ready, (n + 1).n)
                    wait(pe, exp_done, n.n)
                    for t in range(2):
                        o = ps_s[:, t * P:(t + 1) * P]
                        for kd in range(KD):
                            pe.matmul(o, xnT[:, kd, t * P:(t + 1) * P], ctxT[:, kd, t * P:(t + 1) * P],
                                      start=(kd == 0), stop=False)
                        i = pe.matmul(o, batch_of[:, :], bias[:, bass.ds(n.n * 2 + t, 1), :].rearrange("b t m -> b (t m)"),
                                      start=False, stop=True)
                    i.then_inc(scores_ready, 1)
                if third(k):
                    pe.wait_ge(x2n_ready, (m + 1).n)
                    wait(pe, x2nT_ready, m.n)
                    transposes(ps_x2, x2n).then_inc(x2T_done, 1)
                if enters(k):
                    pe.wait_ge(ctx_in[k.slot(2)], 16 * (k.use(2) + 1))
                    wait(pe, ctxT_ready, k.n)
                    transposes(ps_c, ctx_sb[:, k.slot(2), :, :]).then_inc(cT_done, 1)
                if second(k):
                    pe.wait_ge(exp_done, (n + 1).n)
                    wait(pe, pT_ready, n.n)
                    for t in range(2):
                        i = pe.transpose(ps_p[:, t * P:(t + 1) * P], probs[:, t, :], ident[:, :])
                    i.then_inc(pT_done, 1)
                if third(k):
                    pe.wait_ge(x2nT_ready, (m + 1).n)
                    wait(pe, lg_ready, m.n)
                    for kd in range(KD):
                        i = pe.matmul(ps_l[0:E, 0:2 * P], router[:, kd, :], x2nT[:, kd, :],
                                      start=(kd == 0), stop=(kd == KD - 1))
                    i.then_inc(logits_done, 1)
                if second(k):
                    pe.wait_ge(pT_ready, (n + 1).n)
                    wait(pe, x2_done, n.n)
                    for t in range(2):
                        i = pe.matmul(ps_r[:, t, :], probsT[:, t, :], ctx_sb[:, n.slot(2), t, :], start=True, stop=True)
                    i.then_inc(readout_done, 1)
                if third(k):
                    apart(pe, (lg_ready, (m + 1).n), (expz_done, m.n))
                    for t in range(2):
                        i = pe.transpose(ps_b[:, t * E:(t + 1) * E], logits[:, t * P:(t + 1) * P], ident[0:E, 0:E])
                    i.then_inc(lb_done, 1)
                if enters(k):
                    pe.wait_ge(xn_ready, (k + 1).n)
                    wait(pe, xnT_ready, k.n)
                    transposes(ps_x, xn).then_inc(xT_done, 1)

            pe.wait_ge(small_in, 48)
            pairs(pe, turn)

            pe.wait_ge(route_ready, PAIRS)
            oh = onehot[:, :, :].rearrange("p e t -> p (e t)")
            pe.matmul(ps_x[:, 0, 0:E * T], ones_b[:, :], oh, start=True, stop=True)
            pe.matmul(ps_c[:, 0, 0:E * T], tri_b[:, :], oh, start=True, stop=True).then_inc(counts_done, 1)
            pe.wait_ge(aval_ready, 1)
            for t in range(T):
                pe.wait_ge(b_ready, 4 * t // T + 1)
                i = pe.matmul(ps_s[:, 0:SL], b_hot[:, t, :], a_val[:, t, :], start=(t == 0), stop=(t == T - 1))
            i.then_inc(slots_done, 1)

            def x_t(j):
                pe.wait_ge(fx_ready, (j + 1).n)
                wait(pe, xlo_ready, j.n)
                for k in range(KD):
                    i = pe.transpose(pf_x[:, k, :], fx[:, k * P:(k + 1) * P], ident[:, :])
                i.then_inc(fxT_done, 1)

            def half(bank, e, m, ready):
                for k in range(KD):
                    at = bass.ds(e * (2 * WM) + (m * WM + k * I), I)
                    pe.matmul(bank[:, :], fxT_hi[:, k, :], w_hi[:, at], start=(k == 0), stop=False)
                    pe.matmul(bank[:, :], fxT_hi[:, k, :], w_lo[:, at], start=False, stop=False)
                    i = pe.matmul(bank[:, :], fxT_lo[:, k, :], w_hi[:, at], start=False, stop=(k == KD - 1))
                i.then_inc(ready, 1)

            def expert(j):
                return pe.value_load(tile_expert[0:1, bass.ds(j.n, 1)], min_val=0, max_val=E - 1)

            def down(j):
                apart(pe, (hT_ready, (j + 1).n), (y_ready, j.n))
                e = expert(j)
                for k in range(KI):
                    i = pe.matmul(pf_y[:, 0:D], hT[:, k, :], w_dn[:, bass.ds(e * WDN + k * D, D)],
                                  start=(k == 0), stop=(k == KI - 1))
                i.then_inc(down_done, 1)

            pe.wait_ge(expert_ready, 1)
            x_t(At(None, 0, 0))

            def tile(j):
                apart(pe, (xlo_ready, (j + 1).n))
                e = expert(j)
                wait(pe, silu_done, j.n)
                half(pf_g, e, 0, g_done)
                wait(pe, h_ready, j.n)
                half(pf_u, e, 1, u_done)
                if not last(j):
                    x_t(j + 1)
                if j.i is not None or j.c > 0:
                    down(j - 1)
                pe.wait_ge(h_ready, (j + 1).n)
                wait(pe, hT_ready, j.n)
                for k in range(KI):
                    i = pe.transpose(pf_h[:, k, :], h[:, k * P:(k + 1) * P], ident[:, :])
                i.then_inc(hT_done, 1)
                if j.i is None and j.c == 0:
                    pe.wait_ge(down_in, 16 * E)

            tiles(pe, tile)
            down(At(None, 0, SLOTS - 1))


_INS = ["x", "ctx_2048", "mask_BxS2_bk0", "g_xattn", "g_ffn", "L0_ffn_router_w", "L0_ffn_gate_w",
        "L0_ffn_up_w", "L0_ffn_down_w"]


def kernel(**inputs):
    import numpy as np
    import concourse.bacc as bacc
    from concourse.bass_utils import run_bass_kernel_spmd

    nc = bacc.Bacc("TRN2", target_bir_lowering=False, num_devices=1)
    arrays, args = {}, []
    for name in _INS:
        v = np.ascontiguousarray(inputs[name])
        arrays[f"in_{name}"] = v
        args.append(nc.dram_tensor(f"in_{name}", v.shape, mybir.dt.from_np(v.dtype), kind="ExternalInput").ap())
    out = nc.dram_tensor("out", inputs["x"].shape, F32, kind="ExternalOutput").ap()
    gated_block(nc, *args, out)
    r = run_bass_kernel_spmd(nc, [arrays], core_ids=[0])
    return r.results[0]["out"]
```

```python
from contextlib import ExitStack

import concourse.bass as bass
from concourse import mybir
from concourse.alu_op_type import AluOpType as ALU

F32 = mybir.dt.float32
F32R = mybir.dt.float32r
BF16 = mybir.dt.bfloat16
F16 = mybir.dt.float16
I32 = mybir.dt.int32
U8 = mybir.dt.uint8
ACT = mybir.ActivationFunctionType
AX = mybir.AxisListType

P = 128
NEG = -1e30
EPS = 1e-5


class Steps:

    def __init__(self, engine, sem):
        self.engine, self.sem, self.base, self.n = engine, sem, 0, 0

    def done(self, instruction, apart=None):
        instruction.then_inc(self.sem, 1)
        self.n += 1
        if apart:
            return apart(self.engine, (self.sem, self.base + self.n))
        self.engine.wait_ge(self.sem, self.base + self.n)

    def mark(self, instruction):
        instruction.then_inc(self.sem, 1)
        self.n += 1
        return self.base + self.n

    def enter(self, i, per_turn):
        self.start, self.base, self.n = self.base + self.n, self.base + self.n + i * per_turn, 0

    def leave(self, turns, per_turn):
        assert self.n == per_turn, (self.n, per_turn)
        self.base, self.n = self.start + turns * per_turn, 0


def apart_after(met):
    def apart(engine, *waits):
        waits = [(s, v if isinstance(v, int) else engine.to_reg(v)) for s, v in waits]
        engine.wait_ge(met, 1)
        for s, v in waits:
            wait(engine, s, v)
    return apart


class At:

    def __init__(self, i, of, c):
        self.i, self.of, self.c = i, of, c

    def __add__(self, d):
        return At(self.i, self.of, self.c + d)

    def __sub__(self, d):
        return At(self.i, self.of, self.c - d)

    @property
    def n(self):
        return self.c if self.i is None else self.i * self.of + self.c

    def slot(self, ring):
        return self.c % ring

    def use(self, ring):
        return self.c // ring if self.i is None else self.i * (self.of // ring) + self.c // ring


def wait(engine, sem, value):
    if not isinstance(value, int) or value > 0:
        engine.wait_ge(sem, value)


def gated_block(nc, x, ctx, mask, g_xattn, g_ffn, router_w, gate_w, up_w, down_w, out):
    B, S, D = x.shape
    E, _, I = gate_w.shape
    TOK = B * S
    T = TOK // P
    PAIRS = T // 2
    KD, KI = D // P, I // P
    SLOTS = (TOK - E) // P + E
    SL = SLOTS + 1
    COLS = D + 4
    WM = KD * I
    WDN = KI * D
    GROUPS = 8
    SCALE = 1.0 / float(D) ** 0.5

    x_v = x.rearrange("b s d -> (b s) d").rearrange("(t p) d -> p t d", p=P)
    ctx_v = ctx.rearrange("b s d -> (b s) d").rearrange("(t p) d -> p t d", p=P)
    out_v = out.rearrange("b s d -> (b s) d")
    mask_v = mask.rearrange("(t b) m -> b t m", b=2)
    table = nc.dram_tensor("rows_by_token", [TOK, COLS], F32).ap()
    table_v = table.rearrange("(t p) c -> p t c", p=P)

    def gate_up(w, e):
        return w[bass.ds(e, 1), :, :].rearrange("a (k p) n -> p (a k) n", p=P)

    with ExitStack() as stack:
        def sb(name, shape, dt=F32, on=stack):
            return on.enter_context(nc.sbuf_tensor(name, shape, dt))

        def pb(name, on, shape=(P, 512)):
            return on.enter_context(nc.psum_tensor(name, list(shape), F32))

        def sem(name):
            return stack.enter_context(nc.semaphore(name))

        w_hi = sb("w_hi", [P, E * 2 * WM], F32R)
        w_lo = sb("w_lo", [P, E * 2 * WM], F32R)
        ident = sb("ident", [P, P])
        xg = sb("xg", [P, 4, COLS])
        slot_idx = sb("slot_idx", [P, SL], I32)
        gather_now = sb("gather_now", [P, 4], I32)
        scatter_now = sb("scatter_now", [P, 2], I32)
        tile_expert = sb("tile_expert", [1, SL], I32)

        stage = sb("stage", [P, 2, 2, WM])
        ones_b = sb("ones_b", [P, P], BF16)
        tri_b = sb("tri_b", [P, P], BF16)
        onehot = sb("onehot", [P, E, T], BF16)
        tanhs = sb("tanhs", [P, 2])
        ones8 = sb("ones8", [P, E])
        rev8 = sb("rev8", [P, E])
        keep = sb("keep", [P, E, T])
        tok_m = sb("tok_m", [P, T], F16)
        iota_h = sb("iota_h", [P, SL], F16)
        iota_p = sb("iota_p", [P, P], F16)
        iota_sl = sb("iota_sl", [P, SL])
        thr = sb("thr", [P, T])
        route = sb("route", [P, T, E])
        best = sb("best", [P, T])

        one = ExitStack()
        a = lambda name, shape, dt=F32: sb(name, shape, dt, one)
        row = a("row", [P, T, COLS])
        bias = a("bias", [2, T, P], BF16)
        any2 = a("any2", [2, T], BF16)
        batch_of = a("batch_of", [2, P], BF16)
        gates = a("gates", [P, 2])
        coef_x = a("coef_x", [P, T])
        bn1 = a("bn1", [P, 2, 6])
        mv1 = a("mv1", [P, 2, 2])
        ve1 = a("ve1", [P, 2])
        rs1 = a("rs1", [P, 2])
        rmax = a("rmax", [P, 2])
        nmax = a("nmax", [P, 2])
        rsum = a("rsum", [P, 2])
        ctx_sb = a("ctx_sb", [P, 2, 2, D])
        xn = a("xn", [P, 2, D])
        xnT = a("xnT", [P, KD, 2 * P])
        ctxT = a("ctxT", [P, KD, 2 * P])
        probs = a("probs", [P, 2, P])
        probsT = a("probsT", [P, 2, P])
        x2n = a("x2n", [P, 2, D])
        x2nT = a("x2nT", [P, KD, 2 * P])
        router = a("router", [P, KD, E])
        bn2 = a("bn2", [P, 2, 6])
        mv2 = a("mv2", [P, 2, 2])
        ve2 = a("ve2", [P, 2])
        minus_half = a("minus_half", [P, 2])
        cs = a("cs", [P, 2])
        ez = a("ez", [P, 2, E])
        sig = a("sig", [P, 2, E])
        top = a("top", [P, 2])
        mask2 = x2nT[0:2, :, :].rearrange("b k t -> b (k t)").bitcast(U8).rearrange("b (t m) -> b t m", t=T)
        mask_words = x2nT[0:2, :, :].bitcast(I32)
        ps_x = pb("ps_x", one, (P, KD, 2 * P))
        ps_c = pb("ps_c", one, (P, KD, 2 * P))
        ps_s = pb("ps_s", one)
        ps_p = pb("ps_p", one)
        ps_r = pb("ps_r", one, (P, 2, D))
        ps_x2 = pb("ps_x2", one, (P, KD, 2 * P))
        ps_l = pb("ps_l", one, (P, 2, 256))
        ps_b = pb("ps_b", one)
        one.close()

        w_dn = sb("w_dn", [P, E * WDN])
        fx = sb("fx", [P, D])
        fxT_hi = sb("fxT_hi", [P, KD, P], F32R)
        fxT_lo = sb("fxT_lo", [P, KD, P], F32R)
        sil = sb("sil", [P, I])
        h = sb("h", [P, I])
        hT = sb("hT", [P, KI, P])
        yo = sb("yo", [P, 2, D])
        upto = sb("upto", [P, E, T])
        rank = sb("rank", [P, E, T])
        over = sb("over", [P, E, T])
        ntile = sb("ntile", [P, E])
        tend = sb("tend", [P, E])
        tstart = sb("tstart", [P, E])
        pos = sb("pos", [P, T])
        pos_i = sb("pos_i", [P, T], I32)
        pos_a = sb("pos_a", [P, T], I32)
        a_of = sb("a_of", [P, T], F16)
        b_of = sb("b_of", [P, T], F16)
        a_hot = sb("a_hot", [P, T, SL], F16)
        a_val = sb("a_val", [P, T, SL], F16)
        b_hot = sb("b_hot", [P, T, P], F16)
        past = sb("past", [1, SL, E])
        past_n = sb("past_n", [1, SL])
        pf_g = pb("pf_g", stack)
        pf_u = pb("pf_u", stack)
        pf_x = pb("pf_x", stack, (P, KD, P))
        pf_h = pb("pf_h", stack, (P, KI, P))
        pf_y = pb("pf_y", stack)

        x_in = [sem(f"x_in{s}") for s in range(2)]
        ctx_in = [sem(f"ctx_in{s}") for s in range(2)]
        small_in = sem("small_in")
        mask_in = sem("mask_in")
        gate_in = [sem(f"gate_in{s}") for s in range(2)]
        up_in = [sem(f"up_in{s}") for s in range(2)]
        down_in = sem("down_in")
        row_out = [sem(f"row_out{s}") for s in range(2)]
        gathered = [sem(f"gathered{s}") for s in range(4)]
        stored = [sem(f"stored{s}") for s in range(2)]
        mask_clear = sem("mask_clear")
        keep_ready = sem("keep_ready")
        const_ready = sem("const_ready")
        bias_ready = sem("bias_ready")
        any_ready = sem("any_ready")
        tanh_ready = sem("tanh_ready")
        valid_ready = sem("valid_ready")
        (scores_ready, negmax_ready, exp_done, pT_done, pT_ready, readout_done, x2_done,
         var1_ready, rstd1_ready, xn_ready, xT_done, xnT_ready, cT_done, ctxT_ready,
         var2_ready, rstd2_ready, x2n_ready, x2T_done, x2nT_ready, logits_done,
         expz_done, route_ready, whi_ready, wlo_ready) = [sem(n) for n in (
            "scores_ready", "negmax_ready", "exp_done", "pT_done", "pT_ready", "readout_done",
            "x2_done", "var1_ready", "rstd1_ready", "xn_ready", "xT_done", "xnT_ready", "cT_done",
            "ctxT_ready", "var2_ready", "rstd2_ready", "x2n_ready", "x2T_done", "x2nT_ready",
            "logits_done", "expz_done", "route_ready", "whi_ready",
            "wlo_ready")]
        nb2_ready = sem("nb2_ready")
        cs_ready = sem("cs_ready")
        onehot_ready = sem("onehot_ready")
        counts_done, ahot_ready, aval_ready, hot_ready, slots_done, idx_ready, expert_ready = [
            sem(n) for n in ("counts_done", "ahot_ready", "aval_ready", "hot_ready", "slots_done",
                             "idx_ready", "expert_ready")]
        (g_done, u_done, silu_done, h_ready, hT_done, hT_ready, down_done, y_ready, fx_ready,
         fxT_done, xhi_ready, xlo_ready, idx_copied) = [sem(n) for n in (
            "g_done", "u_done", "silu_done", "h_ready", "hT_done", "hT_ready", "down_done",
            "y_ready", "fx_ready", "fxT_done", "xhi_ready", "xlo_ready", "idx_copied")]
        sidx_copied = sem("sidx_copied")
        dve_steps, act_steps, pool_steps = sem("dve_steps"), sem("act_steps"), sem("pool_steps")

        apart = apart_after(const_ready)
        block = stack.enter_context(nc.Block())

        DEPTH = 3
        TURNS = (PAIRS - DEPTH) // 2
        FTURNS = (SLOTS - 3) // 4

        def pairs(engine, body, steps=None, per_turn=0):
            for k in range(DEPTH):
                body(At(None, 0, k))
            with engine.Fori(0, TURNS) as i:
                if steps:
                    steps.enter(i, per_turn)
                for u in range(2):
                    body(At(i, 2, DEPTH + u))
            if steps:
                steps.leave(TURNS, per_turn)
            for k in range(DEPTH + 2 * TURNS, PAIRS + DEPTH):
                body(At(None, 0, k))

        def at_stage(k, d):
            return k.i is not None or 0 <= k.c - d < PAIRS

        def tiles(engine, body):
            body(At(None, 0, 0))
            with engine.Fori(0, FTURNS) as i:
                for u in range(4):
                    body(At(i, 4, 1 + u))
            for j in range(1 + 4 * FTURNS, SLOTS):
                body(At(None, 0, j))

        def last(j):
            return j.i is None and j.c == SLOTS - 1

        @block.sync
        def _(sp):
            def load_x(k):
                wait(sp, x_in[k.slot(2)], 16 * k.use(2))
                sp.dma_start(row[:, bass.ds(k.n * 2, 2), 0:D], x_v[:, bass.ds(k.n * 2, 2), :]).then_inc(x_in[k.slot(2)], 16)

            def load_ctx(k):
                wait(sp, readout_done, (k - 1).n)
                sp.dma_start(ctx_sb[:, k.slot(2), :, :], ctx_v[:, bass.ds(k.n * 2, 2), :]).then_inc(ctx_in[k.slot(2)], 16)

            def load_matrix(k, m):
                wait(sp, wlo_ready, 2 * (k - 2).n + m + 1)
                s = stage[:, k.slot(2), m, :].rearrange("p (k n) -> p k n", k=KD)
                sp.dma_start(s, gate_up((gate_w, up_w)[m], k.n)).then_inc((gate_in, up_in)[m][k.slot(2)], 16)

            def store_rows(k):
                sp.wait_ge(route_ready, (k + 1).n)
                wait(sp, row_out[k.slot(2)], 16 * k.use(2))
                sp.dma_start(table_v[:, bass.ds(k.n * 2, 2), :], row[:, bass.ds(k.n * 2, 2), :]).then_inc(row_out[k.slot(2)], 16)

            first = At(None, 0, 0)
            load_x(first)
            load_ctx(first)
            sp.wait_ge(mask_clear, 1)
            for b in range(2):
                sp.dma_start(mask2[b:b + 1, :, b * S:(b + 1) * S], mask_v[b:b + 1, :, :]).then_inc(mask_in, 16)
            sp.dma_start(gates[:, 0:1], g_xattn.partition_broadcast(P)).then_inc(small_in, 16)
            sp.dma_start(gates[:, 1:2], g_ffn.partition_broadcast(P)).then_inc(small_in, 16)
            load_x(first + 1)
            load_ctx(first + 1)
            load_matrix(first, 0)
            sp.dma_start(router[:, :, :], router_w.rearrange("(k p) e -> p k e", p=P)).then_inc(small_in, 16)
            load_matrix(first, 1)

            def turn(k):
                if k.i is not None or k.c + 2 < PAIRS:
                    load_x(k + 2)
                if k.i is not None or k.c + 1 < PAIRS:
                    load_matrix(k + 1, 0)
                    if k.i is not None or k.c > 0:
                        load_ctx(k + 1)
                    load_matrix(k + 1, 1)
                if at_stage(k, 3):
                    store_rows(k - 3)

            def load_down(e):
                sp.dma_start(w_dn[:, e * WDN:(e + 1) * WDN].rearrange("p (k n) -> p k n", k=KI),
                             down_w[e, :, :].rearrange("(k p) n -> p k n", p=P)).then_inc(down_in, 16)

            for c in range(DEPTH):
                turn(At(None, 0, c))
            turns = (PAIRS - 2 - DEPTH) // 2
            with sp.Fori(0, turns) as i:
                for u in range(2):
                    turn(At(i, 2, DEPTH + u))
            for c in range(DEPTH + 2 * turns, PAIRS + DEPTH):
                turn(At(None, 0, c))
                if c in (PAIRS - 1, PAIRS + 1):
                    pairs_out = (4, 6)[c > PAIRS]
                    for s in range(2):
                        sp.wait_ge(row_out[s], 16 * (pairs_out // 2))
                    for e in ((0, 1), (2,))[c > PAIRS]:
                        load_down(e)
                if c == PAIRS:
                    sp.wait_ge(readout_done, PAIRS)
                    for e in range(5, E):
                        load_down(e)
            for s in range(2):
                sp.wait_ge(row_out[s], 16 * (PAIRS // 2))
            for e in (3, 4):
                load_down(e)

        @block.gpsimd
        def _(pool):
            steps = Steps(pool, pool_steps)
            pool.memset(mask_words, 0).then_inc(mask_clear, 1)
            pool.memset(ident[:, :], 0.0)
            pool.memset(ones_b[:, :], 1.0)
            pool.memset(tri_b[:, :], 1.0)
            pool.memset(batch_of[:, :], 1.0)
            pool.memset(minus_half[:, :], -0.5)
            steps.done(pool.memset(ones8[:, :], 1.0))
            pool.affine_select(out=ident[:, :], in_=ident[:, :], compare_op=ALU.not_equal, fill=1.0,
                               base=0, pattern=[[-1, P]], channel_multiplier=1)
            pool.affine_select(out=tri_b[:, :], in_=tri_b[:, :], compare_op=ALU.is_gt, fill=0.0,
                               base=0, pattern=[[1, P]], channel_multiplier=-1)
            steps.done(pool.affine_select(out=batch_of[:, :], in_=batch_of[:, :], compare_op=ALU.is_ge, fill=0.0,
                                          base=0, pattern=[[1, P]], channel_multiplier=-S))
            pool.affine_select(out=batch_of[:, :], in_=batch_of[:, :], compare_op=ALU.is_ge, fill=0.0,
                               base=S - 1, pattern=[[-1, P]], channel_multiplier=S)
            loose = dict(allow_small_or_imprecise_dtypes=True)
            pool.iota(rev8[:, :], [[-1, E]], base=E, channel_multiplier=0, **loose).then_inc(const_ready, 1)
            steps.done(pool.memset(keep[:, :, :], 1.0))
            pool.affine_select(out=keep[:, :, :], in_=keep[:, :, :], compare_op=ALU.not_equal, fill=0.0,
                               base=0, pattern=[[0, E], [1, T]], channel_multiplier=0)
            pool.iota(thr[:, :], [[P, T]], base=0, channel_multiplier=0, **loose)
            pool.iota(iota_sl[:, :], [[1, SL]], base=0, channel_multiplier=0, **loose)
            pool.iota(iota_h[:, :], [[1, SL]], base=0, channel_multiplier=0, **loose)
            pool.iota(iota_p[:, :], [[1, P]], base=0, channel_multiplier=0, **loose)
            pool.memset(xg[:, :, :], 0.0)
            pool.iota(tok_m[:, :], [[P, T]], base=-TOK, channel_multiplier=1, **loose).then_inc(keep_ready, 1)

            def split_lo(k, m):
                apart(pool, (whi_ready, 2 * k.n + m + 1))
                at = bass.ds(k.n * (2 * WM) + m * WM, WM)
                pool.tensor_tensor(w_lo[:, at], stage[:, k.slot(2), m, :], w_hi[:, at].bitcast(F32),
                                   ALU.subtract).then_inc(wlo_ready, 1)

            pool.wait_ge(const_ready, 1)

            def turn(k):
                r = k - 2
                if at_stage(k, 2):
                    apart(pool, (var2_ready, (r + 1).n))
                    pool.tensor_tensor(row[:, bass.ds(r.n * 2, 2), D], ve2[:, :], minus_half[:, :],
                                       ALU.pow).then_inc(rstd2_ready, 1)
                if at_stage(k, 0):
                    pool.wait_ge(var1_ready, (k + 1).n)
                    wait(pool, xn_ready, k.n)
                    pool.tensor_tensor(rs1[:, :], ve1[:, :], minus_half[:, :], ALU.pow).then_inc(rstd1_ready, 1)
                if at_stage(k, 1):
                    split_lo(k - 1, 0)
                    split_lo(k - 1, 1)

            pairs(pool, turn)
            def index_of(j, now, copied, count):
                if j.i is None:
                    return slot_idx[:, j.c:j.c + 1]
                pool.tensor_copy(now, slot_idx[:, bass.ds(j.n, 1)]).then_inc(copied, 1)
                apart(pool, (copied, count))
                return now

            def gather(j):
                s = j.slot(4)
                apart(pool, (y_ready, (j - 3).n))
                at = index_of(j, gather_now[:, s:s + 1], idx_copied, (j - 3).n)
                pool.indirect_dma_start(
                    xg[:, s, :], None, table, bass.IndirectOffsetOnAxis(ap=at, axis=0),
                    bounds_check=TOK - 1, oob_is_err=False).then_inc(gathered[s], 16)

            def scatter(j):
                s = j.slot(2)
                apart(pool, (y_ready, (j + 1).n), (stored[s], 16 * j.use(2)))
                at = index_of(j, scatter_now[:, s:s + 1], sidx_copied, (j + 1).n)
                pool.indirect_dma_start(
                    out_v, bass.IndirectOffsetOnAxis(ap=at, axis=0),
                    yo[:, s, :], None, bounds_check=TOK - 1, oob_is_err=False).then_inc(stored[s], 16)

            pool.wait_ge(ahot_ready, 1)
            pool.tensor_tensor(a_val[:, :, :], a_hot[:, :, :],
                               tok_m[:, :].unsqueeze(2).to_broadcast([P, T, SL]), ALU.mult).then_inc(aval_ready, 1)
            for s in range(2):
                pool.wait_ge(row_out[s], 16 * (PAIRS // 2))
            pool.wait_ge(idx_ready, 1)
            for c in range(3):
                gather(At(None, 0, c))

            def turn_f(j):
                if j.i is not None or j.c + 3 < SLOTS:
                    gather(j + 3)
                if j.i is not None or j.c > 0:
                    scatter(j - 1)

            turn_f(At(None, 0, 0))
            turns = (SLOTS - 4) // 4
            with pool.Fori(0, turns) as i:
                for u in range(4):
                    turn_f(At(i, 4, 1 + u))
            for j in range(1 + 4 * turns, SLOTS):
                turn_f(At(None, 0, j))
            scatter(At(None, 0, SLOTS - 1))
            for s in range(2):
                pool.wait_ge(stored[s], 16 * ((SLOTS + 1 - s) // 2))

        @block.scalar
        def _(act):
            act.wait_ge(small_in, 48)
            act.activation(tanhs[:, :], gates[:, :], ACT.Tanh).then_inc(tanh_ready, 1)

            def split_hi(k, m):
                act.wait_ge((gate_in, up_in)[m][k.slot(2)], 16 * (k.use(2) + 1))
                at = bass.ds(k.n * (2 * WM) + m * WM, WM)
                act.activation(w_hi[:, at], stage[:, k.slot(2), m, :], ACT.Copy).then_inc(whi_ready, 1)

            def turn(k):
                n, r, m = k - 1, k - 2, k - 3
                if at_stage(k, 1):
                    act.wait_ge(negmax_ready, (n + 1).n)
                    wait(act, pT_done, n.n)
                    wait(act, cs_ready, n.n)
                    for t in range(2):
                        e = act.activation(probs[:, t, :], ps_s[:, t * P:(t + 1) * P], ACT.Exp, bias=nmax[:, t:t + 1],
                                           scale=SCALE, accum_out=rsum[:, t:t + 1])
                    e.then_inc(exp_done, 1)
                if at_stage(k, 3):
                    act.wait_ge(logits_done, (m + 1).n)
                    wait(act, route_ready, m.n)
                    act.activation(ez[:, :, :], ps_l[:, :, 0:E], ACT.Exp, scale=-1.0).then_inc(expz_done, 1)
                if at_stage(k, 1):
                    act.wait_ge(pT_done, (n + 1).n)
                    wait(act, readout_done, n.n)
                    act.activation(probsT[:, :, :], ps_p[:, 0:2 * P].rearrange("p (t m) -> p t m", t=2),
                                   ACT.Copy).then_inc(pT_ready, 1)
                if at_stage(k, 0):
                    act.wait_ge(cT_done, (k + 1).n)
                    wait(act, scores_ready, k.n)
                    act.activation(ctxT[:, :, :], ps_c[:, :, :], ACT.Copy).then_inc(ctxT_ready, 1)
                if at_stage(k, 2):
                    act.wait_ge(nb2_ready, (r + 1).n)
                    wait(act, x2T_done, r.n)
                    for t in range(2):
                        q = row[:, bass.ds(r.n * 2 + t, 1), :].rearrange("p a c -> p (a c)")
                        i = act.activation(x2n[:, t, :], q[:, 0:D], ACT.Identity, bias=q[:, D + 1:D + 2],
                                           scale=q[:, D:D + 1])
                    i.then_inc(x2n_ready, 1)
                if at_stage(k, 0):
                    act.wait_ge(xT_done, (k + 1).n)
                    act.activation(xnT[:, :, :], ps_x[:, :, :], ACT.Copy).then_inc(xnT_ready, 1)
                if at_stage(k, 2):
                    act.wait_ge(x2T_done, (r + 1).n)
                    wait(act, logits_done, r.n)
                    act.activation(x2nT[:, :, :], ps_x2[:, :, :], ACT.Copy).then_inc(x2nT_ready, 1)
                if at_stage(k, 0):
                    split_hi(k, 0)
                    split_hi(k, 1)

            pairs(act, turn)

            def x_hi(j):
                act.wait_ge(fxT_done, (j + 1).n)
                wait(act, u_done, j.n)
                wait(act, xlo_ready, j.n)
                act.activation(fxT_hi[:, :, :], pf_x[:, :, :], ACT.Copy).then_inc(xhi_ready, 1)

            x_hi(At(None, 0, 0))

            def tile(j):
                act.wait_ge(g_done, (j + 1).n)
                wait(act, h_ready, j.n)
                act.activation(sil[:, :], pf_g[:, :], ACT.Silu).then_inc(silu_done, 1)
                if not last(j):
                    x_hi(j + 1)
                act.wait_ge(hT_done, (j + 1).n)
                wait(act, down_done, j.n)
                act.activation(hT[:, :, :], pf_h[:, :, :], ACT.Copy).then_inc(hT_ready, 1)

            tiles(act, tile)

        @block.vector
        def _(dve):
            steps = Steps(dve, dve_steps)
            done = steps.done
            def ln_stats(k, bn, mv, ve, ready):
                for t in range(2):
                    i = dve.bn_stats(bn[:, t, :], row[:, bass.ds(k.n * 2 + t, 1), 0:D].rearrange("p a c -> p (a c)"))
                done(i, apart)
                for t in range(2):
                    i = dve.bn_aggr(mv[:, t, :], bn[:, t, :])
                done(i)
                dve.tensor_scalar(ve[:, :], mv[:, :, 1], EPS, None, ALU.add).then_inc(ready, 1)

            def first_best(m0, m1):
                n, at = 2 * (m1 - m0), slice(2 * m0, 2 * m1)
                tokens = lambda z: z[:, at].unsqueeze(2).to_broadcast([P, n, E])
                numbers = rev8[:, :].unsqueeze(1).to_broadcast([P, n, E])
                dve.wait_ge(route_ready, m1)
                done(dve.tensor_reduce(best[:, at], route[:, at, :], axis=AX.X, op=ALU.max))
                done(dve.tensor_tensor(route[:, at, :], route[:, at, :], tokens(best), ALU.is_equal))
                done(dve.tensor_tensor(route[:, at, :], route[:, at, :], numbers, ALU.mult))
                done(dve.tensor_reduce(best[:, at], route[:, at, :], axis=AX.X, op=ALU.max))
                dve.tensor_tensor(onehot[:, :, at].rearrange("p e t -> p t e"), numbers, tokens(best),
                                  ALU.is_equal).then_inc(onehot_ready, 1)

            def turn(k):
                n, r, m = k - 1, k - 2, k - 3
                if k.i is None and k.c == PAIRS + DEPTH - 1:
                    first_best(0, PAIRS - 1)
                if at_stage(k, 0):
                    dve.wait_ge(x_in[k.slot(2)], 16 * (k.use(2) + 1))
                    ln_stats(k, bn1, mv1, ve1, var1_ready)
                if k.i is None and k.c == 0:
                    dve.wait_ge(mask_in, 32)
                    dve.tensor_scalar(bias[:, :, :], mask2[:, :, :], 1.0, -NEG, ALU.subtract,
                                      ALU.mult).then_inc(bias_ready, 1)
                if k.i is None and k.c == 1:
                    dve.wait_ge(valid_ready, 1)
                    dve.wait_ge(tanh_ready, 1)
                    done(dve.tensor_scalar(coef_x[:, :], ps_b[:, 0:T], tanhs[:, 0:1], None, ALU.mult))
                if at_stage(k, 1):
                    dve.wait_ge(exp_done, (n + 1).n)
                    done(dve.reciprocal(cs[:, :], rsum[:, :]))
                    dve.tensor_tensor(cs[:, :], cs[:, :], coef_x[:, bass.ds(n.n * 2, 2)], ALU.mult).then_inc(cs_ready, 1)
                if at_stage(k, 2):
                    q = row[:, bass.ds(r.n * 2, 2), :]
                    dve.wait_ge(rstd2_ready, (r + 1).n)
                    dve.scalar_tensor_tensor(q[:, :, D + 1], mv2[:, :, 0], -1.0, q[:, :, D], ALU.mult,
                                             ALU.mult).then_inc(nb2_ready, 1)
                if at_stage(k, 0):
                    dve.wait_ge(rstd1_ready, (k + 1).n)
                    wait(dve, xT_done, k.n)
                    for t in range(2):
                        i = dve.tensor_scalar(xn[:, t, :], row[:, bass.ds(k.n * 2 + t, 1), 0:D].rearrange("p a c -> p (a c)"),
                                              mv1[:, t, 0:1], rs1[:, t:t + 1], ALU.subtract, ALU.mult)
                    i.then_inc(xn_ready, 1)
                if k.i is None and k.c == 0:
                    dve.tensor_reduce(any2[:, :], mask2[:, :, :], axis=AX.X, op=ALU.max).then_inc(any_ready, 1)
                if at_stage(k, 1):
                    dve.wait_ge(cs_ready, (n + 1).n)
                    dve.wait_ge(readout_done, (n + 1).n)
                    for t in range(2):
                        q = row[:, bass.ds(n.n * 2 + t, 1), 0:D].rearrange("p a c -> p (a c)")
                        i = dve.scalar_tensor_tensor(q, ps_r[:, t, :], cs[:, t:t + 1], q, ALU.mult, ALU.add)
                    i.then_inc(x2_done, 1)
                    apart(dve, (x2_done, (n + 1).n))
                    ln_stats(n, bn2, mv2, ve2, var2_ready)
                if at_stage(k, 0):
                    dve.wait_ge(scores_ready, (k + 1).n)
                    done(dve.tensor_reduce(rmax[:, :], ps_s[:, 0:2 * P].rearrange("p (t m) -> p t m", t=2),
                                           axis=AX.X, op=ALU.max))
                    dve.tensor_scalar(nmax[:, :], rmax[:, :], -SCALE, None, ALU.mult).then_inc(negmax_ready, 1)
                if at_stage(k, 3):
                    mt = bass.ds(m.n * 2, 2)
                    dve.wait_ge(expz_done, (m + 1).n)
                    done(dve.tensor_scalar(sig[:, :, :], ez[:, :, :], 1.0, None, ALU.add))
                    done(dve.reciprocal(sig[:, :, :], sig[:, :, :]))
                    done(dve.tensor_reduce(top[:, :], sig[:, :, :], axis=AX.X, op=ALU.max))
                    dve.tensor_copy(route[:, mt, :], sig[:, :, :])
                    dve.tensor_scalar(row[:, mt, D + 2], top[:, :], tanhs[:, 1:2], None, ALU.mult).then_inc(route_ready, 1)

            done(dve.memset(row[:, :, D + 3], 0.0))
            dve.wait_ge(const_ready, 1)
            pairs(dve, turn, steps, 2 * (2 + 1 + 2 + 1 + 3))
            first_best(PAIRS - 1, PAIRS)

            dve.wait_ge(counts_done, 1)
            dve.wait_ge(keep_ready, 1)
            flat = lambda z: z[:, :, :].rearrange("p e t -> p (e t)")
            counts = ps_x[:, 0, 0:E * T]
            mark, met = steps.mark, lambda *steps_: [dve.wait_ge(dve_steps, v) for v in steps_]
            done(dve.tensor_tensor_scan(flat(upto), flat(keep), counts, 0.0, ALU.mult, ALU.add))
            over_at = mark(dve.tensor_tensor(over[:, :, :], upto[:, :, T - 1:T].to_broadcast([P, E, T]),
                                             thr[:, :].unsqueeze(1).to_broadcast([P, E, T]), ALU.is_gt))
            rank_at = mark(dve.tensor_tensor(flat(rank), flat(upto), counts, ALU.subtract))
            met(over_at)
            ntile_at = mark(dve.tensor_reduce(ntile[:, :], over[:, :, :], axis=AX.X, op=ALU.add))
            met(rank_at)
            rank_at = mark(dve.tensor_tensor(flat(rank), flat(rank), ps_c[:, 0, 0:E * T], ALU.add))
            met(ntile_at)
            done(dve.tensor_tensor_scan(tend[:, :], ones8[:, :], ntile[:, :], 0.0, ALU.mult, ALU.add))
            done(dve.tensor_tensor(tstart[:, :], tend[:, :], ntile[:, :], ALU.subtract))
            rank_at = mark(dve.scalar_tensor_tensor(rank[:, :, :], tstart[:, :].unsqueeze(2).to_broadcast([P, E, T]),
                                                    float(P), rank[:, :, :], ALU.mult, ALU.add))
            past_at = mark(dve.tensor_tensor(past[:, :, :], iota_sl[0:1, :].unsqueeze(2).to_broadcast([1, SL, E]),
                                             tend[0:1, :].unsqueeze(1).to_broadcast([1, SL, E]), ALU.is_ge))
            met(rank_at)
            rank_at = mark(dve.tensor_tensor(rank[:, :, :], rank[:, :, :], onehot[:, :, :], ALU.mult))
            met(past_at)
            past_at = mark(dve.tensor_reduce(past_n[:, :], past[:, :, :], axis=AX.X, op=ALU.add))
            met(rank_at)
            pos_at = mark(dve.tensor_reduce(pos[:, :], rank[:, :, :].rearrange("p e t -> p t e"), axis=AX.X, op=ALU.add))
            met(past_at)
            dve.tensor_scalar(tile_expert[:, :], past_n[:, :], float(E - 1), None, ALU.min).then_inc(expert_ready, 1)
            met(pos_at)
            done(dve.tensor_copy(pos_i[:, :], pos[:, :]))
            shift = P.bit_length() - 1
            done(dve.tensor_scalar(pos_a[:, :], pos_i[:, :], shift, None, ALU.logical_shift_right))
            dve.tensor_copy(a_of[:, :], pos_a[:, :])
            done(dve.scalar_tensor_tensor(b_of[:, :], pos_a[:, :], -float(P), pos[:, :], ALU.mult, ALU.add))
            dve.tensor_tensor(a_hot[:, :, :], iota_h[:, :].unsqueeze(1).to_broadcast([P, T, SL]),
                                   a_of[:, :].unsqueeze(2).to_broadcast([P, T, SL]), ALU.is_equal).then_inc(ahot_ready, 1)
            for q in range(GROUPS):
                t0, t1 = q * T // GROUPS, (q + 1) * T // GROUPS
                dve.tensor_tensor(b_hot[:, t0:t1, :], iota_p[:, :].unsqueeze(1).to_broadcast([P, t1 - t0, P]),
                                  b_of[:, t0:t1].unsqueeze(2).to_broadcast([P, t1 - t0, P]),
                                  ALU.is_equal).then_inc(hot_ready, 1)
            dve.wait_ge(slots_done, 1)
            dve.tensor_scalar(slot_idx[:, :], ps_s[:, 0:SL], float(TOK), None, ALU.add).then_inc(idx_ready, 1)

            def normalised(j):
                dve.wait_ge(gathered[j.slot(4)], 16 * (j.use(4) + 1))
                wait(dve, fxT_done, j.n)
                r = xg[:, j.slot(4), :]
                dve.tensor_scalar(fx[:, :], r[:, 0:D], r[:, D:D + 1], r[:, D + 1:D + 2],
                                  ALU.mult, ALU.add).then_inc(fx_ready, 1)

            def x_lo(j):
                dve.wait_ge(xhi_ready, (j + 1).n)
                wait(dve, u_done, j.n)
                dve.tensor_tensor(fxT_lo[:, :, :], pf_x[:, :, :], fxT_hi[:, :, :].bitcast(F32),
                                  ALU.subtract).then_inc(xlo_ready, 1)

            def output(j):
                dve.wait_ge(down_done, (j + 1).n)
                wait(dve, stored[j.slot(2)], 16 * j.use(2))
                r = xg[:, j.slot(4), :]
                dve.scalar_tensor_tensor(yo[:, j.slot(2), :], pf_y[:, 0:D], r[:, D + 2:D + 3], r[:, 0:D],
                                         ALU.mult, ALU.add).then_inc(y_ready, 1)

            first = At(None, 0, 0)
            normalised(first)
            x_lo(first)
            normalised(first + 1)

            def tile(j):
                dve.wait_ge(silu_done, (j + 1).n)
                dve.wait_ge(u_done, (j + 1).n)
                wait(dve, hT_done, j.n)
                dve.tensor_tensor(h[:, :], sil[:, :], pf_u[:, :], ALU.mult).then_inc(h_ready, 1)
                if not last(j):
                    x_lo(j + 1)
                if j.i is not None or j.c > 0:
                    output(j - 1)
                if not last(j) and not last(j + 1):
                    normalised(j + 2)

            tiles(dve, tile)
            output(At(None, 0, SLOTS - 1))

        @block.tensor
        def _(pe):
            pe.wait_ge(const_ready, 1)

            def transposes(dst, src):
                for t in range(2):
                    for k in range(KD):
                        i = pe.transpose(dst[:, k, t * P:(t + 1) * P], src(t, slice(k * P, (k + 1) * P)), ident[:, :])
                return i

            def turn(k):
                n, r = k - 1, k - 2
                if at_stage(k, 1):
                    pe.wait_ge(exp_done, (n + 1).n)
                    wait(pe, pT_ready, n.n)
                    for t in range(2):
                        i = pe.transpose(ps_p[:, t * P:(t + 1) * P], probs[:, t, :], ident[:, :])
                    i.then_inc(pT_done, 1)
                if at_stage(k, 0):
                    pe.wait_ge(ctx_in[k.slot(2)], 16 * (k.use(2) + 1))
                    wait(pe, ctxT_ready, k.n)
                    transposes(ps_c, lambda t, c: ctx_sb[:, k.slot(2), t, c]).then_inc(cT_done, 1)
                if at_stage(k, 1):
                    pe.wait_ge(pT_ready, (n + 1).n)
                    wait(pe, x2_done, n.n)
                    for t in range(2):
                        i = pe.matmul(ps_r[:, t, :], probsT[:, t, :], ctx_sb[:, n.slot(2), t, :], start=True, stop=True)
                    i.then_inc(readout_done, 1)
                if at_stage(k, 0):
                    pe.wait_ge(xn_ready, (k + 1).n)
                    wait(pe, xnT_ready, k.n)
                    transposes(ps_x, lambda t, c: xn[:, t, c]).then_inc(xT_done, 1)
                if at_stage(k, 2):
                    pe.wait_ge(x2n_ready, (r + 1).n)
                    wait(pe, x2nT_ready, r.n)
                    transposes(ps_x2, lambda t, c: x2n[:, t, c]).then_inc(x2T_done, 1)
                if at_stage(k, 0):
                    pe.wait_ge(xnT_ready, (k + 1).n)
                    pe.wait_ge(ctxT_ready, (k + 1).n)
                    wait(pe, exp_done, k.n)
                    if k.i is None and k.c == 0:
                        pe.wait_ge(bias_ready, 1)
                    for t in range(2):
                        o = ps_s[:, t * P:(t + 1) * P]
                        for kd in range(KD):
                            pe.matmul(o, xnT[:, kd, t * P:(t + 1) * P], ctxT[:, kd, t * P:(t + 1) * P],
                                      start=(kd == 0), stop=False)
                        i = pe.matmul(o, batch_of[:, :], bias[:, bass.ds(k.n * 2 + t, 1), :].rearrange("b t m -> b (t m)"),
                                      start=False, stop=True)
                    i.then_inc(scores_ready, 1)
                if k.i is None and k.c == 0:
                    pe.wait_ge(any_ready, 1)
                    pe.matmul(ps_b[:, 0:T], batch_of[:, :], any2[:, :], start=True, stop=True).then_inc(valid_ready, 1)
                if at_stage(k, 2):
                    pe.wait_ge(x2nT_ready, (r + 1).n)
                    wait(pe, expz_done, r.n)
                    if k.i is None and k.c == 2:
                        pe.wait_ge(small_in, 48)
                    for t in range(2):
                        for kd in range(KD):
                            i = pe.matmul(ps_l[:, t, 0:E], x2nT[:, kd, t * P:(t + 1) * P], router[:, kd, :],
                                          start=(kd == 0), stop=(kd == KD - 1))
                    i.then_inc(logits_done, 1)

            pairs(pe, turn)

            pe.wait_ge(onehot_ready, 2)
            oh = onehot[:, :, :].rearrange("p e t -> p (e t)")
            pe.matmul(ps_x[:, 0, 0:E * T], ones_b[:, :], oh, start=True, stop=True)
            pe.matmul(ps_c[:, 0, 0:E * T], tri_b[:, :], oh, start=True, stop=True).then_inc(counts_done, 1)
            pe.wait_ge(aval_ready, 1)
            for t in range(T):
                pe.wait_ge(hot_ready, GROUPS * t // T + 1)
                i = pe.matmul(ps_s[:, 0:SL], b_hot[:, t, :], a_val[:, t, :], start=(t == 0), stop=(t == T - 1))
            i.then_inc(slots_done, 1)

            def x_t(j):
                pe.wait_ge(fx_ready, (j + 1).n)
                wait(pe, xlo_ready, j.n)
                for k in range(KD):
                    i = pe.transpose(pf_x[:, k, :], fx[:, k * P:(k + 1) * P], ident[:, :])
                i.then_inc(fxT_done, 1)

            def half(bank, e, m, ready):
                for k in range(KD):
                    at = bass.ds(e * (2 * WM) + (m * WM + k * I), I)
                    pe.matmul(bank[:, :], fxT_hi[:, k, :], w_hi[:, at], start=(k == 0), stop=False)
                    pe.matmul(bank[:, :], fxT_hi[:, k, :], w_lo[:, at], start=False, stop=False)
                    i = pe.matmul(bank[:, :], fxT_lo[:, k, :], w_hi[:, at], start=False, stop=(k == KD - 1))
                i.then_inc(ready, 1)

            def expert(j):
                return pe.value_load(tile_expert[0:1, bass.ds(j.n, 1)], min_val=0, max_val=E - 1)

            def down(j):
                e = expert(j)
                apart(pe, (hT_ready, (j + 1).n), (y_ready, j.n))
                for k in range(KI):
                    i = pe.matmul(pf_y[:, 0:D], hT[:, k, :], w_dn[:, bass.ds(e * WDN + k * D, D)],
                                  start=(k == 0), stop=(k == KI - 1))
                i.then_inc(down_done, 1)

            pe.wait_ge(expert_ready, 1)
            x_t(At(None, 0, 0))

            def tile(j):
                e = expert(j)
                apart(pe, (xlo_ready, (j + 1).n))
                wait(pe, silu_done, j.n)
                half(pf_g, e, 0, g_done)
                wait(pe, h_ready, j.n)
                half(pf_u, e, 1, u_done)
                if not last(j):
                    x_t(j + 1)
                if j.i is not None or j.c > 0:
                    down(j - 1)
                pe.wait_ge(h_ready, (j + 1).n)
                wait(pe, hT_ready, j.n)
                for k in range(KI):
                    i = pe.transpose(pf_h[:, k, :], h[:, k * P:(k + 1) * P], ident[:, :])
                i.then_inc(hT_done, 1)
                if j.i is None and j.c == 0:
                    pe.wait_ge(down_in, 16 * E)

            tiles(pe, tile)
            down(At(None, 0, SLOTS - 1))


_INS = ["x", "ctx_2048", "mask_BxS2_bk0", "g_xattn", "g_ffn", "L0_ffn_router_w", "L0_ffn_gate_w",
        "L0_ffn_up_w", "L0_ffn_down_w"]


def kernel(**inputs):
    import numpy as np
    import concourse.bacc as bacc
    from concourse.bass_utils import run_bass_kernel_spmd

    nc = bacc.Bacc("TRN2", target_bir_lowering=False, num_devices=1)
    arrays, args = {}, []
    for name in _INS:
        v = np.ascontiguousarray(inputs[name])
        arrays[f"in_{name}"] = v
        args.append(nc.dram_tensor(f"in_{name}", v.shape, mybir.dt.from_np(v.dtype), kind="ExternalInput").ap())
    out = nc.dram_tensor("out", inputs["x"].shape, F32, kind="ExternalOutput").ap()
    gated_block(nc, *args, out)
    r = run_bass_kernel_spmd(nc, [arrays], core_ids=[0])
    return r.results[0]["out"]
```

```python
from contextlib import ExitStack

import concourse.bass as bass
from concourse import mybir
from concourse.alu_op_type import AluOpType as ALU

F32 = mybir.dt.float32
F32R = mybir.dt.float32r
BF16 = mybir.dt.bfloat16
F16 = mybir.dt.float16
I32 = mybir.dt.int32
U8 = mybir.dt.uint8
ACT = mybir.ActivationFunctionType
AX = mybir.AxisListType

P = 128
NEG = -1e30
EPS = 1e-5


class Steps:

    def __init__(self, engine, sem):
        self.engine, self.sem, self.base, self.n = engine, sem, 0, 0

    def done(self, instruction, apart=None):
        instruction.then_inc(self.sem, 1)
        self.n += 1
        if apart:
            return apart(self.engine, (self.sem, self.base + self.n))
        self.engine.wait_ge(self.sem, self.base + self.n)

    def mark(self, instruction):
        instruction.then_inc(self.sem, 1)
        self.n += 1
        return self.base + self.n

    def enter(self, i, per_turn):
        self.start, self.base, self.n = self.base + self.n, self.base + self.n + i * per_turn, 0

    def leave(self, turns, per_turn):
        assert self.n == per_turn, (self.n, per_turn)
        self.base, self.n = self.start + turns * per_turn, 0


def apart_after(met):
    def apart(engine, *waits):
        waits = [(s, v if isinstance(v, int) else engine.to_reg(v)) for s, v in waits]
        engine.wait_ge(met, 1)
        for s, v in waits:
            wait(engine, s, v)
    return apart


class At:

    def __init__(self, i, of, c):
        self.i, self.of, self.c = i, of, c

    def __add__(self, d):
        return At(self.i, self.of, self.c + d)

    def __sub__(self, d):
        return At(self.i, self.of, self.c - d)

    @property
    def n(self):
        return self.c if self.i is None else self.i * self.of + self.c

    def slot(self, ring):
        return self.c % ring

    def use(self, ring):
        return self.c // ring if self.i is None else self.i * (self.of // ring) + self.c // ring


def wait(engine, sem, value):
    if not isinstance(value, int) or value > 0:
        engine.wait_ge(sem, value)


def gated_block(nc, x, ctx, mask, g_xattn, g_ffn, router_w, gate_w, up_w, down_w, out):
    B, S, D = x.shape
    E, _, I = gate_w.shape
    TOK = B * S
    T = TOK // P
    PAIRS = T // 2
    KD, KI = D // P, I // P
    SLOTS = (TOK - E) // P + E
    SL = SLOTS + 1
    COLS = D + 4
    WM = KD * I
    WDN = KI * D
    GROUPS = 8
    WARM = 10
    SCALE = 1.0 / float(D) ** 0.5

    x_v = x.rearrange("b s d -> (b s) d").rearrange("(t p) d -> p t d", p=P)
    ctx_v = ctx.rearrange("b s d -> (b s) d").rearrange("(t p) d -> p t d", p=P)
    out_v = out.rearrange("b s d -> (b s) d")
    mask_v = mask.rearrange("(t b) m -> b t m", b=2)
    table = nc.dram_tensor("rows_by_token", [TOK, COLS], F32).ap()
    table_v = table.rearrange("(t p) c -> p t c", p=P)

    def gate_up(w, e):
        return w[bass.ds(e, 1), :, :].rearrange("a (k p) n -> p (a k) n", p=P)

    with ExitStack() as stack:
        def sb(name, shape, dt=F32, on=stack):
            return on.enter_context(nc.sbuf_tensor(name, shape, dt))

        def pb(name, on, shape=(P, 512)):
            return on.enter_context(nc.psum_tensor(name, list(shape), F32))

        def sem(name):
            return stack.enter_context(nc.semaphore(name))

        w_hi = sb("w_hi", [P, E * 2 * WM], F32R)
        w_lo = sb("w_lo", [P, E * 2 * WM], F32R)
        ident = sb("ident", [P, P])
        xg = sb("xg", [P, 4, COLS])
        slot_idx = sb("slot_idx", [P, SL], I32)
        gather_now = sb("gather_now", [P, 4], I32)
        scatter_now = sb("scatter_now", [P, 2], I32)
        tile_expert = sb("tile_expert", [1, SL], I32)
        tiles_used = sb("tiles_used", [1, 1], I32)

        one = ExitStack()
        a = lambda name, shape, dt=F32: sb(name, shape, dt, one)
        upto = a("upto", [P, E, T])
        rank = a("rank", [P, E, T])
        over = a("over", [P, E, T])
        ntile = a("ntile", [P, E])
        tend = a("tend", [P, E])
        tstart = a("tstart", [P, E])
        pos = a("pos", [P, T])
        pos_i = a("pos_i", [P, T], I32)
        pos_a = a("pos_a", [P, T], I32)
        a_of = a("a_of", [P, T], F16)
        b_of = a("b_of", [P, T], F16)
        a_hot = a("a_hot", [P, T, SL], F16)
        a_val = a("a_val", [P, T, SL], F16)
        b_hot = a("b_hot", [P, T, P], F16)
        past = a("past", [1, SL, E])
        past_n = a("past_n", [1, SL])
        ones_b = a("ones_b", [P, P], BF16)
        tri_b = a("tri_b", [P, P], BF16)
        onehot = a("onehot", [P, E, T], BF16)
        tanhs = a("tanhs", [P, 2])
        ones8 = a("ones8", [P, E])
        rev8 = a("rev8", [P, E])
        keep = a("keep", [P, E, T])
        tok_m = a("tok_m", [P, T], F16)
        iota_h = a("iota_h", [P, SL], F16)
        iota_p = a("iota_p", [P, P], F16)
        iota_sl = a("iota_sl", [P, SL])
        thr = a("thr", [P, T])
        route = a("route", [P, T, E])
        best = a("best", [P, T])
        row = a("row", [P, T, COLS])
        bias = a("bias", [2, T, P], BF16)
        any2 = a("any2", [2, T], BF16)
        batch_of = a("batch_of", [2, P], BF16)
        gates = a("gates", [P, 2])
        coef_x = a("coef_x", [P, T])
        bn1 = a("bn1", [P, 2, 6])
        mv1 = a("mv1", [P, 2, 2])
        ve1 = a("ve1", [P, 2])
        rs1 = a("rs1", [P, 2])
        rmax = a("rmax", [P, 2])
        nmax = a("nmax", [P, 2])
        rsum = a("rsum", [P, 2])
        ctx_sb = a("ctx_sb", [P, 2, 2, D])
        xn = a("xn", [P, 2, 2, D])
        xnT = a("xnT", [P, KD, 2 * P])
        ctxT = a("ctxT", [P, KD, 2 * P])
        probs = a("probs", [P, 2, P])
        probsT = a("probsT", [P, 2, P])
        x2n = a("x2n", [P, 2, D])
        x2nT = a("x2nT", [P, KD, 2 * P])
        router = a("router", [P, KD, E])
        bn2 = a("bn2", [P, 2, 6])
        mv2 = a("mv2", [P, 2, 2])
        ve2 = a("ve2", [P, 2])
        minus_half = a("minus_half", [P, 2])
        cs = a("cs", [P, 2])
        ez = a("ez", [P, 2, E])
        sig = a("sig", [P, 2, E])
        top = a("top", [P, 2])
        stage = a("stage", [P, 2, 2, WM])
        mask2 = x2nT[0:2, :, :].rearrange("b k t -> b (k t)").bitcast(U8).rearrange("b (t m) -> b t m", t=T)
        mask_words = x2nT[0:2, :, :].bitcast(I32)
        ps_x = pb("ps_x", one, (P, KD, 2 * P))
        ps_c = pb("ps_c", one, (P, KD, 2 * P))
        ps_s = pb("ps_s", one)
        ps_p = pb("ps_p", one)
        ps_r = pb("ps_r", one, (P, 2, D))
        ps_x2 = pb("ps_x2", one, (P, KD, 2 * P))
        ps_l = pb("ps_l", one, (P, 2, 256))
        ps_b = pb("ps_b", one)
        one.close()

        fx = sb("fx", [P, D])
        fxT_hi = sb("fxT_hi", [P, KD, P], F32R)
        fxT_lo = sb("fxT_lo", [P, KD, P], F32R)
        h = sb("h", [P, I])
        hT_hi = sb("hT_hi", [P, KI, P], F32R)
        hT_lo = sb("hT_lo", [P, KI, P], F32R)
        yo = sb("yo", [P, 2, D])
        d_lo = sb("d_lo", [P, E * WDN], F32R)
        d_hi = sb("d_hi", [P, E * WDN], F32R)
        pf_g = pb("pf_g", stack)
        pf_u = pb("pf_u", stack)
        pf_x = pb("pf_x", stack, (P, KD, P))
        pf_h = pb("pf_h", stack, (P, KI, P))
        pf_y = pb("pf_y", stack)

        x_in = [sem(f"x_in{s}") for s in range(2)]
        ctx_in = [sem(f"ctx_in{s}") for s in range(2)]
        small_in = sem("small_in")
        mask_in = sem("mask_in")
        gate_in = [sem(f"gate_in{s}") for s in range(2)]
        up_in = [sem(f"up_in{s}") for s in range(2)]
        down_in = [sem(f"down_in{e}") for e in range(E)]
        d_hi_ready, d_lo_ready, d_lo_ready_dve = [sem(n) for n in ("d_hi_ready", "d_lo_ready", "d_lo_ready_dve")]
        row_out = [sem(f"row_out{s}") for s in range(2)]
        gathered = [sem(f"gathered{s}") for s in range(4)]
        stored = [sem(f"stored{s}") for s in range(2)]
        mask_clear = sem("mask_clear")
        keep_ready = sem("keep_ready")
        const_ready = sem("const_ready")
        bias_ready = sem("bias_ready")
        any_ready = sem("any_ready")
        tanh_ready = sem("tanh_ready")
        valid_ready = sem("valid_ready")
        (scores_ready, negmax_ready, exp_done, pT_done, pT_ready, readout_done, x2_done,
         var1_ready, rstd1_ready, xn_ready, xT_done, xnT_ready, cT_done, ctxT_ready,
         var2_ready, rstd2_ready, x2n_ready, x2T_done, x2nT_ready, logits_done,
         expz_done, route_ready) = [sem(n) for n in (
            "scores_ready", "negmax_ready", "exp_done", "pT_done", "pT_ready", "readout_done",
            "x2_done", "var1_ready", "rstd1_ready", "xn_ready", "xT_done", "xnT_ready", "cT_done",
            "ctxT_ready", "var2_ready", "rstd2_ready", "x2n_ready", "x2T_done", "x2nT_ready",
            "logits_done", "expz_done", "route_ready")]
        whi_ready = [sem(n) for n in ("gate_hi_ready", "up_hi_ready")]
        wlo_ready = [sem(n) for n in ("gate_lo_ready", "up_lo_ready")]
        nb2_ready = sem("nb2_ready")
        cs_ready = sem("cs_ready")
        onehot_ready = sem("onehot_ready")
        counts_done, ahot_ready, aval_ready, hot_ready, slots_done, idx_ready, expert_ready = [
            sem(n) for n in ("counts_done", "ahot_ready", "aval_ready", "hot_ready", "slots_done",
                             "idx_ready", "expert_ready")]
        used_ready = sem("used_ready")
        (g_done, u_done, silu_done, h_ready, hT_done, hT_ready, down_done, y_ready, fx_ready, hTlo_ready,
         fxT_done, xhi_ready, xlo_ready, idx_copied) = [sem(n) for n in (
            "g_done", "u_done", "silu_done", "h_ready", "hT_done", "hT_ready", "down_done",
            "y_ready", "fx_ready", "hTlo_ready", "fxT_done", "xhi_ready", "xlo_ready", "idx_copied")]
        sidx_copied = sem("sidx_copied")
        dve_steps, pool_steps = sem("dve_steps"), sem("pool_steps")

        apart = apart_after(const_ready)
        SPLIT_ORDER = (6, 7, 4, 5, 0, 1, 2, 3)

        def down_lo(engine, e, ready):
            at = slice(e * WDN, (e + 1) * WDN)
            engine.wait_ge(d_hi_ready, SPLIT_ORDER.index(e) + 1)
            engine.tensor_tensor(d_lo[:, at], d_lo[:, at].bitcast(F32), d_hi[:, at].bitcast(F32),
                                 ALU.subtract).then_inc(ready, 1)

        block = stack.enter_context(nc.Block())

        DEPTH = 4
        TURNS = (PAIRS - DEPTH) // 2
        ALWAYS = 1 + TOK // P
        assert (ALWAYS - 1) % 4 == 0

        def pairs(engine, body, steps=None, per_turn=0):
            for k in range(DEPTH):
                body(At(None, 0, k))
            with engine.Fori(0, TURNS) as i:
                if steps:
                    steps.enter(i, per_turn)
                for u in range(2):
                    body(At(i, 2, DEPTH + u))
            if steps:
                steps.leave(TURNS, per_turn)
            for k in range(DEPTH + 2 * TURNS, PAIRS + DEPTH):
                body(At(None, 0, k))

        def at_stage(k, d):
            return k.i is not None or 0 <= k.c - d < PAIRS

        def tiles(engine, body, end, read_used):
            body(At(None, 0, 0))
            with engine.Fori(0, (ALWAYS - 1) // 4) as i:
                for u in range(4):
                    body(At(i, 4, 1 + u))
            used = read_used()
            for j in range(ALWAYS, SLOTS + 1):
                if j < SLOTS:
                    with engine.If(used > j):
                        body(At(None, 0, j))
                if end:
                    with engine.If(used == j):
                        end(At(None, 0, j - 1))

        def read_used(engine):
            engine.wait_ge(used_ready, 1)
            return engine.value_load(tiles_used[0:1, 0:1], min_val=ALWAYS, max_val=SLOTS)

        def last(j):
            return j.i is None and j.c == SLOTS - 1

        @block.sync
        def _(sp):
            def load_x(k):
                wait(sp, x_in[k.slot(2)], 16 * k.use(2))
                sp.dma_start(row[:, bass.ds(k.n * 2, 2), 0:D], x_v[:, bass.ds(k.n * 2, 2), :]).then_inc(x_in[k.slot(2)], 16)

            def load_ctx(k):
                wait(sp, readout_done, (k - 1).n)
                sp.dma_start(ctx_sb[:, k.slot(2), :, :], ctx_v[:, bass.ds(k.n * 2, 2), :]).then_inc(ctx_in[k.slot(2)], 16)

            def load_matrix(k, m):
                wait(sp, wlo_ready[m], (k - 1).n)
                s = stage[:, k.slot(2), m, :].rearrange("p (k n) -> p k n", k=KD)
                sp.dma_start(s, gate_up((gate_w, up_w)[m], k.n)).then_inc((gate_in, up_in)[m][k.slot(2)], 16)

            def store_rows(k):
                sp.wait_ge(route_ready, (k + 1).n)
                wait(sp, row_out[k.slot(2)], 16 * k.use(2))
                sp.dma_start(table_v[:, bass.ds(k.n * 2, 2), :], row[:, bass.ds(k.n * 2, 2), :]).then_inc(row_out[k.slot(2)], 16)

            first = At(None, 0, 0)
            load_x(first)
            load_ctx(first)
            sp.wait_ge(mask_clear, 1)
            for b in range(2):
                sp.dma_start(mask2[b:b + 1, :, b * S:(b + 1) * S], mask_v[b:b + 1, :, :]).then_inc(mask_in, 16)
            sp.dma_start(gates[:, 0:1], g_xattn.partition_broadcast(P)).then_inc(small_in, 16)
            sp.dma_start(gates[:, 1:2], g_ffn.partition_broadcast(P)).then_inc(small_in, 16)
            load_x(first + 1)
            load_ctx(first + 1)
            load_matrix(first, 1)
            sp.dma_start(router[:, :, :], router_w.rearrange("(k p) e -> p k e", p=P)).then_inc(small_in, 16)
            load_matrix(first, 0)
            load_matrix(first + 1, 1)

            def turn(k):
                if k.i is not None or k.c + 2 < PAIRS:
                    load_x(k + 2)
                if k.i is not None or 2 <= k.c < PAIRS:
                    load_matrix(k, 1)
                    load_ctx(k)
                if k.i is not None or 1 <= k.c - 1 < PAIRS:
                    load_matrix(k - 1, 0)
                if at_stage(k, 4):
                    store_rows(k - 4)

            def load_down(e):
                sp.dma_start(d_lo[:, e * WDN:(e + 1) * WDN].bitcast(F32).rearrange("p (k n) -> p k n", k=KI),
                             down_w[e, :, :].rearrange("(k p) n -> p k n", p=P)).then_inc(down_in[e], 16)

            for c in range(DEPTH):
                turn(At(None, 0, c))
            turns = (PAIRS - 2 - DEPTH) // 2
            with sp.Fori(0, turns) as i:
                for u in range(2):
                    turn(At(i, 2, DEPTH + u))
            for c in range(DEPTH + 2 * turns, PAIRS + DEPTH):
                turn(At(None, 0, c))
                if c == PAIRS + 1:
                    sp.wait_ge(readout_done, PAIRS)
                    for e in (6, 7, 4, 5):
                        load_down(e)
                if c in (PAIRS - 1, PAIRS + 1):
                    pairs_out, e = ((4, 0), (6, 1))[c > PAIRS]
                    for s in range(2):
                        sp.wait_ge(row_out[s], 16 * (pairs_out // 2))
                    load_down(e)
            for s in range(2):
                sp.wait_ge(row_out[s], 16 * (PAIRS // 2))
            for e in (2, 3):
                load_down(e)

        @block.gpsimd
        def _(pool):
            steps = Steps(pool, pool_steps)
            pool.memset(mask_words, 0).then_inc(mask_clear, 1)
            pool.memset(ident[:, :], 0.0)
            pool.memset(ones_b[:, :], 1.0)
            pool.memset(tri_b[:, :], 1.0)
            pool.memset(batch_of[:, :], 1.0)
            pool.memset(minus_half[:, :], -0.5)
            steps.done(pool.memset(ones8[:, :], 1.0))
            pool.affine_select(out=ident[:, :], in_=ident[:, :], compare_op=ALU.not_equal, fill=1.0,
                               base=0, pattern=[[-1, P]], channel_multiplier=1)
            pool.affine_select(out=tri_b[:, :], in_=tri_b[:, :], compare_op=ALU.is_gt, fill=0.0,
                               base=0, pattern=[[1, P]], channel_multiplier=-1)
            steps.done(pool.affine_select(out=batch_of[:, :], in_=batch_of[:, :], compare_op=ALU.is_ge, fill=0.0,
                                          base=0, pattern=[[1, P]], channel_multiplier=-S))
            pool.affine_select(out=batch_of[:, :], in_=batch_of[:, :], compare_op=ALU.is_ge, fill=0.0,
                               base=S - 1, pattern=[[-1, P]], channel_multiplier=S)
            loose = dict(allow_small_or_imprecise_dtypes=True)
            pool.iota(rev8[:, :], [[-1, E]], base=E, channel_multiplier=0, **loose).then_inc(const_ready, 1)
            steps.done(pool.memset(keep[:, :, :], 1.0))
            pool.affine_select(out=keep[:, :, :], in_=keep[:, :, :], compare_op=ALU.not_equal, fill=0.0,
                               base=0, pattern=[[0, E], [1, T]], channel_multiplier=0)
            pool.iota(thr[:, :], [[P, T]], base=0, channel_multiplier=0, **loose)
            pool.iota(iota_sl[:, :], [[1, SL]], base=0, channel_multiplier=0, **loose)
            pool.iota(iota_h[:, :], [[1, SL]], base=0, channel_multiplier=0, **loose)
            pool.iota(iota_p[:, :], [[1, P]], base=0, channel_multiplier=0, **loose)
            pool.memset(xg[:, :, :], 0.0)
            pool.iota(tok_m[:, :], [[P, T]], base=-TOK, channel_multiplier=1, **loose).then_inc(keep_ready, 1)

            def split_lo(k, m):
                apart(pool, (whi_ready[m], (k + 1).n))
                at = bass.ds(k.n * (2 * WM) + m * WM, WM)
                pool.tensor_tensor(w_lo[:, at], stage[:, k.slot(2), m, :], w_hi[:, at].bitcast(F32),
                                   ALU.subtract).then_inc(wlo_ready[m], 1)

            pool.wait_ge(const_ready, 1)

            def turn(k):
                m = k - 3
                if at_stage(k, 2):
                    split_lo(k - 2, 1)
                if at_stage(k, 3):
                    apart(pool, (var2_ready, (m + 1).n))
                    pool.tensor_tensor(row[:, bass.ds(m.n * 2, 2), D], ve2[:, :], minus_half[:, :],
                                       ALU.pow).then_inc(rstd2_ready, 1)
                if at_stage(k, 0):
                    pool.wait_ge(var1_ready, (k + 1).n)
                    wait(pool, xn_ready, k.n)
                    pool.tensor_tensor(rs1[:, :], ve1[:, :], minus_half[:, :], ALU.pow).then_inc(rstd1_ready, 1)
                if at_stage(k, 3):
                    split_lo(m, 0)

            pairs(pool, turn)
            def index_of(j, now, copied, count):
                if j.i is None:
                    return slot_idx[:, j.c:j.c + 1]
                pool.tensor_copy(now, slot_idx[:, bass.ds(j.n, 1)]).then_inc(copied, 1)
                apart(pool, (copied, count))
                return now

            def gather(j):
                s = j.slot(4)
                apart(pool, (y_ready, (j - 3).n))
                at = index_of(j, gather_now[:, s:s + 1], idx_copied, (j - 3).n)
                pool.indirect_dma_start(
                    xg[:, s, :], None, table, bass.IndirectOffsetOnAxis(ap=at, axis=0),
                    bounds_check=TOK - 1, oob_is_err=False).then_inc(gathered[s], 16)

            def scatter(j):
                s = j.slot(2)
                apart(pool, (y_ready, (j + 1).n), (stored[s], 16 * j.use(2)))
                at = index_of(j, scatter_now[:, s:s + 1], sidx_copied, (j + 1).n)
                pool.indirect_dma_start(
                    out_v, bass.IndirectOffsetOnAxis(ap=at, axis=0),
                    yo[:, s, :], None, bounds_check=TOK - 1, oob_is_err=False).then_inc(stored[s], 16)

            down_lo(pool, 6, d_lo_ready)
            down_lo(pool, 7, d_lo_ready)
            pool.wait_ge(ahot_ready, 1)
            pool.tensor_tensor(a_val[:, :, :], a_hot[:, :, :],
                               tok_m[:, :].unsqueeze(2).to_broadcast([P, T, SL]), ALU.mult).then_inc(aval_ready, 1)
            down_lo(pool, 4, d_lo_ready)
            for s in range(2):
                pool.wait_ge(row_out[s], 16 * (PAIRS // 2))
            pool.wait_ge(idx_ready, 1)
            for c in range(3):
                gather(At(None, 0, c))

            def turn_f(j):
                if j.i is not None or j.c + 3 < SLOTS:
                    gather(j + 3)
                if j.i is not None or j.c > 0:
                    scatter(j - 1)

            def turn_p(j):
                turn_f(j)
                if j.i is None and j.c == 0:
                    down_lo(pool, 5, d_lo_ready)

            def end(j):
                scatter(j)
                for s in range(2):
                    pool.wait_ge(stored[s], 16 * ((j.c + 2 - s) // 2))
                for s in range(4):
                    pool.wait_ge(gathered[s], 16 * ((min(j.c + 3, SLOTS - 1) + 4 - s) // 4))

            tiles(pool, turn_p, end, lambda: read_used(pool))

        @block.scalar
        def _(act):
            act.wait_ge(small_in, 48)
            act.activation(tanhs[:, :], gates[:, :], ACT.Tanh).then_inc(tanh_ready, 1)

            def split_hi(k, m):
                act.wait_ge((gate_in, up_in)[m][k.slot(2)], 16 * (k.use(2) + 1))
                at = bass.ds(k.n * (2 * WM) + m * WM, WM)
                act.activation(w_hi[:, at], stage[:, k.slot(2), m, :], ACT.Copy).then_inc(whi_ready[m], 1)

            def turn(k):
                n, r, m, z = k - 1, k - 2, k - 3, k - 4
                if at_stage(k, 4):
                    act.wait_ge(x2T_done, (z + 1).n)
                    wait(act, logits_done, z.n)
                    act.activation(x2nT[:, :, :], ps_x2[:, :, :], ACT.Copy).then_inc(x2nT_ready, 1)
                if at_stage(k, 2):
                    act.wait_ge(negmax_ready, (r + 1).n)
                    wait(act, pT_done, r.n)
                    wait(act, cs_ready, r.n)
                    for t in range(2):
                        e = act.activation(probs[:, t, :], ps_s[:, t * P:(t + 1) * P], ACT.Exp, bias=nmax[:, t:t + 1],
                                           scale=SCALE, accum_out=rsum[:, t:t + 1])
                    e.then_inc(exp_done, 1)
                if at_stage(k, 1):
                    act.wait_ge(cT_done, (n + 1).n)
                    wait(act, scores_ready, n.n)
                    act.activation(ctxT[:, :, :], ps_c[:, :, :], ACT.Copy).then_inc(ctxT_ready, 1)
                if at_stage(k, 4):
                    act.wait_ge(logits_done, (z + 1).n)
                    wait(act, route_ready, z.n)
                    act.activation(ez[:, :, :], ps_l[:, :, 0:E], ACT.Exp, scale=-1.0).then_inc(expz_done, 1)
                if at_stage(k, 2):
                    act.wait_ge(pT_done, (r + 1).n)
                    wait(act, readout_done, r.n)
                    act.activation(probsT[:, :, :], ps_p[:, 0:2 * P].rearrange("p (t m) -> p t m", t=2),
                                   ACT.Copy).then_inc(pT_ready, 1)
                if at_stage(k, 1):
                    act.wait_ge(xT_done, (n + 1).n)
                    act.activation(xnT[:, :, :], ps_x[:, :, :], ACT.Copy).then_inc(xnT_ready, 1)
                    split_hi(n, 1)
                if at_stage(k, 3):
                    act.wait_ge(nb2_ready, (m + 1).n)
                    wait(act, x2T_done, m.n)
                    for t in range(2):
                        q = row[:, bass.ds(m.n * 2 + t, 1), :].rearrange("p a c -> p (a c)")
                        i = act.activation(x2n[:, t, :], q[:, 0:D], ACT.Identity, bias=q[:, D + 1:D + 2],
                                           scale=q[:, D:D + 1])
                    i.then_inc(x2n_ready, 1)
                if at_stage(k, 2):
                    split_hi(r, 0)

            def down_hi(e):
                act.wait_ge(down_in[e], 16)
                act.activation(d_hi[:, e * WDN:(e + 1) * WDN], d_lo[:, e * WDN:(e + 1) * WDN].bitcast(F32),
                               ACT.Copy).then_inc(d_hi_ready, 1)

            pairs(act, turn)
            for e in SPLIT_ORDER:
                if e == 4:
                    for m in range(2):
                        act.wait_ge(wlo_ready[m], E)
                if e == 0:
                    act.wait_ge(route_ready, PAIRS)
                down_hi(e)

            def x_hi(j):
                act.wait_ge(fxT_done, (j + 1).n)
                wait(act, u_done, j.n)
                wait(act, xlo_ready, j.n)
                act.activation(fxT_hi[:, :, :], pf_x[:, :, :], ACT.Copy).then_inc(xhi_ready, 1)

            x_hi(At(None, 0, 0))

            def tile(j):
                act.wait_ge(g_done, (j + 1).n)
                wait(act, hT_done, j.n)
                act.activation(h[:, :], pf_g[:, :], ACT.Silu).then_inc(silu_done, 1)
                if not last(j):
                    x_hi(j + 1)
                act.wait_ge(hT_done, (j + 1).n)
                wait(act, down_done, j.n)
                wait(act, hTlo_ready, j.n)
                act.activation(hT_hi[:, :, :], pf_h[:, :, :], ACT.Copy).then_inc(hT_ready, 1)

            tiles(act, tile, None, lambda: read_used(act))

        @block.vector
        def _(dve):
            steps = Steps(dve, dve_steps)
            done = steps.done
            def ln_stats(k, bn, mv, ve, ready):
                for t in range(2):
                    i = dve.bn_stats(bn[:, t, :], row[:, bass.ds(k.n * 2 + t, 1), 0:D].rearrange("p a c -> p (a c)"))
                done(i, apart)
                for t in range(2):
                    i = dve.bn_aggr(mv[:, t, :], bn[:, t, :])
                done(i)
                dve.tensor_scalar(ve[:, :], mv[:, :, 1], EPS, None, ALU.add).then_inc(ready, 1)

            def first_best(m0, m1):
                n, at = 2 * (m1 - m0), slice(2 * m0, 2 * m1)
                tokens = lambda z: z[:, at].unsqueeze(2).to_broadcast([P, n, E])
                numbers = rev8[:, :].unsqueeze(1).to_broadcast([P, n, E])
                dve.wait_ge(route_ready, m1)
                done(dve.tensor_reduce(best[:, at], route[:, at, :], axis=AX.X, op=ALU.max))
                done(dve.tensor_tensor(route[:, at, :], route[:, at, :], tokens(best), ALU.is_equal))
                done(dve.tensor_tensor(route[:, at, :], route[:, at, :], numbers, ALU.mult))
                done(dve.tensor_reduce(best[:, at], route[:, at, :], axis=AX.X, op=ALU.max))
                dve.tensor_tensor(onehot[:, :, at].rearrange("p e t -> p t e"), numbers, tokens(best),
                                  ALU.is_equal).then_inc(onehot_ready, 1)

            def turn(k):
                n, r, m, z = k - 1, k - 2, k - 3, k - 4
                if k.i is None and k.c == PAIRS + DEPTH - 1:
                    first_best(0, PAIRS - 1)
                if at_stage(k, 0):
                    dve.wait_ge(x_in[k.slot(2)], 16 * (k.use(2) + 1))
                    ln_stats(k, bn1, mv1, ve1, var1_ready)
                if k.i is None and k.c == 0:
                    dve.wait_ge(mask_in, 32)
                    dve.tensor_scalar(bias[:, :, :], mask2[:, :, :], 1.0, -NEG, ALU.subtract,
                                      ALU.mult).then_inc(bias_ready, 1)
                if k.i is None and k.c == 2:
                    dve.wait_ge(valid_ready, 1)
                    dve.wait_ge(tanh_ready, 1)
                    done(dve.tensor_scalar(coef_x[:, :], ps_b[:, 0:T], tanhs[:, 0:1], None, ALU.mult))
                if at_stage(k, 2):
                    dve.wait_ge(exp_done, (r + 1).n)
                    done(dve.reciprocal(cs[:, :], rsum[:, :]))
                    dve.tensor_tensor(cs[:, :], cs[:, :], coef_x[:, bass.ds(r.n * 2, 2)], ALU.mult).then_inc(cs_ready, 1)
                if at_stage(k, 3):
                    q = row[:, bass.ds(m.n * 2, 2), :]
                    dve.wait_ge(rstd2_ready, (m + 1).n)
                    dve.scalar_tensor_tensor(q[:, :, D + 1], mv2[:, :, 0], -1.0, q[:, :, D], ALU.mult,
                                             ALU.mult).then_inc(nb2_ready, 1)
                if at_stage(k, 2):
                    dve.wait_ge(cs_ready, (r + 1).n)
                    dve.wait_ge(readout_done, (r + 1).n)
                    for t in range(2):
                        q = row[:, bass.ds(r.n * 2 + t, 1), 0:D].rearrange("p a c -> p (a c)")
                        i = dve.scalar_tensor_tensor(q, ps_r[:, t, :], cs[:, t:t + 1], q, ALU.mult, ALU.add)
                    i.then_inc(x2_done, 1)
                if at_stage(k, 0):
                    dve.wait_ge(rstd1_ready, (k + 1).n)
                    wait(dve, xT_done, (k - 1).n)
                    for t in range(2):
                        i = dve.tensor_scalar(xn[:, k.slot(2), t, :], row[:, bass.ds(k.n * 2 + t, 1), 0:D].rearrange("p a c -> p (a c)"),
                                              mv1[:, t, 0:1], rs1[:, t:t + 1], ALU.subtract, ALU.mult)
                    i.then_inc(xn_ready, 1)
                if k.i is None and k.c == 0:
                    dve.tensor_reduce(any2[:, :], mask2[:, :, :], axis=AX.X, op=ALU.max).then_inc(any_ready, 1)
                if at_stage(k, 1):
                    dve.wait_ge(scores_ready, (n + 1).n)
                    done(dve.tensor_reduce(rmax[:, :], ps_s[:, 0:2 * P].rearrange("p (t m) -> p t m", t=2),
                                           axis=AX.X, op=ALU.max))
                    dve.tensor_scalar(nmax[:, :], rmax[:, :], -SCALE, None, ALU.mult).then_inc(negmax_ready, 1)
                if at_stage(k, 2):
                    apart(dve, (x2_done, (r + 1).n))
                    ln_stats(r, bn2, mv2, ve2, var2_ready)
                if at_stage(k, 4):
                    mt = bass.ds(z.n * 2, 2)
                    dve.wait_ge(expz_done, (z + 1).n)
                    done(dve.tensor_scalar(sig[:, :, :], ez[:, :, :], 1.0, None, ALU.add))
                    done(dve.reciprocal(sig[:, :, :], sig[:, :, :]))
                    done(dve.tensor_reduce(top[:, :], sig[:, :, :], axis=AX.X, op=ALU.max))
                    dve.tensor_copy(route[:, mt, :], sig[:, :, :])
                    dve.tensor_scalar(row[:, mt, D + 2], top[:, :], tanhs[:, 1:2], None, ALU.mult).then_inc(route_ready, 1)

            done(dve.memset(row[:, :, D + 3], 0.0))
            dve.wait_ge(const_ready, 1)
            pairs(dve, turn, steps, 2 * (2 + 1 + 2 + 1 + 3))
            first_best(PAIRS - 1, PAIRS)

            dve.wait_ge(counts_done, 1)
            dve.wait_ge(keep_ready, 1)
            flat = lambda z: z[:, :, :].rearrange("p e t -> p (e t)")
            counts = ps_x[:, 0, 0:E * T]
            mark, met = steps.mark, lambda *steps_: [dve.wait_ge(dve_steps, v) for v in steps_]
            done(dve.tensor_tensor_scan(flat(upto), flat(keep), counts, 0.0, ALU.mult, ALU.add))
            over_at = mark(dve.tensor_tensor(over[:, :, :], upto[:, :, T - 1:T].to_broadcast([P, E, T]),
                                             thr[:, :].unsqueeze(1).to_broadcast([P, E, T]), ALU.is_gt))
            rank_at = mark(dve.tensor_tensor(flat(rank), flat(upto), counts, ALU.subtract))
            met(over_at)
            ntile_at = mark(dve.tensor_reduce(ntile[:, :], over[:, :, :], axis=AX.X, op=ALU.add))
            met(rank_at)
            rank_at = mark(dve.tensor_tensor(flat(rank), flat(rank), ps_c[:, 0, 0:E * T], ALU.add))
            met(ntile_at)
            done(dve.tensor_tensor_scan(tend[:, :], ones8[:, :], ntile[:, :], 0.0, ALU.mult, ALU.add))
            done(dve.tensor_tensor(tstart[:, :], tend[:, :], ntile[:, :], ALU.subtract))
            rank_at = mark(dve.scalar_tensor_tensor(rank[:, :, :], tstart[:, :].unsqueeze(2).to_broadcast([P, E, T]),
                                                    float(P), rank[:, :, :], ALU.mult, ALU.add))
            past_at = mark(dve.tensor_tensor(past[:, :, :], iota_sl[0:1, :].unsqueeze(2).to_broadcast([1, SL, E]),
                                             tend[0:1, :].unsqueeze(1).to_broadcast([1, SL, E]), ALU.is_ge))
            met(rank_at)
            rank_at = mark(dve.tensor_tensor(rank[:, :, :], rank[:, :, :], onehot[:, :, :], ALU.mult))
            met(past_at)
            past_at = mark(dve.tensor_reduce(past_n[:, :], past[:, :, :], axis=AX.X, op=ALU.add))
            met(rank_at)
            pos_at = mark(dve.tensor_reduce(pos[:, :], rank[:, :, :].rearrange("p e t -> p t e"), axis=AX.X, op=ALU.add))
            met(past_at)
            dve.tensor_scalar(tile_expert[:, :], past_n[:, :], float(E - 1), None, ALU.min).then_inc(expert_ready, 1)
            dve.tensor_scalar(tiles_used[:, :], tend[0:1, E - 1:E], float(ALWAYS), None, ALU.max).then_inc(used_ready, 1)
            met(pos_at)
            done(dve.tensor_copy(pos_i[:, :], pos[:, :]))
            shift = P.bit_length() - 1
            done(dve.tensor_scalar(pos_a[:, :], pos_i[:, :], shift, None, ALU.logical_shift_right))
            dve.tensor_copy(a_of[:, :], pos_a[:, :])
            done(dve.scalar_tensor_tensor(b_of[:, :], pos_a[:, :], -float(P), pos[:, :], ALU.mult, ALU.add))
            dve.tensor_tensor(a_hot[:, :, :], iota_h[:, :].unsqueeze(1).to_broadcast([P, T, SL]),
                                   a_of[:, :].unsqueeze(2).to_broadcast([P, T, SL]), ALU.is_equal).then_inc(ahot_ready, 1)
            for q in range(GROUPS):
                t0, t1 = q * T // GROUPS, (q + 1) * T // GROUPS
                dve.tensor_tensor(b_hot[:, t0:t1, :], iota_p[:, :].unsqueeze(1).to_broadcast([P, t1 - t0, P]),
                                  b_of[:, t0:t1].unsqueeze(2).to_broadcast([P, t1 - t0, P]),
                                  ALU.is_equal).then_inc(hot_ready, 1)
            dve.wait_ge(slots_done, 1)
            dve.tensor_scalar(slot_idx[:, :], ps_s[:, 0:SL], float(TOK), None, ALU.add).then_inc(idx_ready, 1)

            down_lo(dve, 0, d_lo_ready_dve)
            down_lo(dve, 1, d_lo_ready_dve)

            def normalised(j):
                dve.wait_ge(gathered[j.slot(4)], 16 * (j.use(4) + 1))
                wait(dve, fxT_done, j.n)
                r = xg[:, j.slot(4), :]
                dve.tensor_scalar(fx[:, :], r[:, 0:D], r[:, D:D + 1], r[:, D + 1:D + 2],
                                  ALU.mult, ALU.add).then_inc(fx_ready, 1)

            def x_lo(j):
                dve.wait_ge(xhi_ready, (j + 1).n)
                wait(dve, u_done, j.n)
                dve.tensor_tensor(fxT_lo[:, :, :], pf_x[:, :, :], fxT_hi[:, :, :].bitcast(F32),
                                  ALU.subtract).then_inc(xlo_ready, 1)

            def output(j):
                dve.wait_ge(down_done, (j + 1).n)
                wait(dve, stored[j.slot(2)], 16 * j.use(2))
                r = xg[:, j.slot(4), :]
                dve.scalar_tensor_tensor(yo[:, j.slot(2), :], pf_y[:, 0:D], r[:, D + 2:D + 3], r[:, 0:D],
                                         ALU.mult, ALU.add).then_inc(y_ready, 1)

            first = At(None, 0, 0)
            normalised(first)
            x_lo(first)
            normalised(first + 1)
            down_lo(dve, 2, d_lo_ready_dve)
            down_lo(dve, 3, d_lo_ready_dve)

            def tile(j):
                dve.wait_ge(silu_done, (j + 1).n)
                dve.wait_ge(u_done, (j + 1).n)
                dve.tensor_tensor(h[:, :], h[:, :], pf_u[:, :], ALU.mult).then_inc(h_ready, 1)
                if not last(j):
                    x_lo(j + 1)
                if j.i is not None or j.c > 0:
                    output(j - 1)
                dve.wait_ge(hT_ready, (j + 1).n)
                dve.tensor_tensor(hT_lo[:, :, :], pf_h[:, :, :], hT_hi[:, :, :].bitcast(F32),
                                  ALU.subtract).then_inc(hTlo_ready, 1)
                if not last(j) and not last(j + 1):
                    normalised(j + 2)

            tiles(dve, tile, output, lambda: read_used(dve))

        @block.tensor
        def _(pe):
            pe.wait_ge(const_ready, 1)

            def transposes(dst, src):
                for t in range(2):
                    for k in range(KD):
                        i = pe.transpose(dst[:, k, t * P:(t + 1) * P], src(t, slice(k * P, (k + 1) * P)), ident[:, :])
                return i

            def turn(k):
                n, r, z = k - 1, k - 2, k - 4
                if at_stage(k, 4):
                    pe.wait_ge(x2n_ready, (z + 1).n)
                    wait(pe, x2nT_ready, z.n)
                    transposes(ps_x2, lambda t, c: x2n[:, t, c]).then_inc(x2T_done, 1)
                if at_stage(k, 1):
                    pe.wait_ge(ctx_in[n.slot(2)], 16 * (n.use(2) + 1))
                    wait(pe, ctxT_ready, n.n)
                    transposes(ps_c, lambda t, c: ctx_sb[:, n.slot(2), t, c]).then_inc(cT_done, 1)
                if at_stage(k, 4):
                    pe.wait_ge(x2nT_ready, (z + 1).n)
                    wait(pe, expz_done, z.n)
                    if k.i is None and k.c == 4:
                        pe.wait_ge(small_in, 48)
                    for t in range(2):
                        for kd in range(KD):
                            i = pe.matmul(ps_l[:, t, 0:E], x2nT[:, kd, t * P:(t + 1) * P], router[:, kd, :],
                                          start=(kd == 0), stop=(kd == KD - 1))
                    i.then_inc(logits_done, 1)
                if at_stage(k, 2):
                    pe.wait_ge(exp_done, (r + 1).n)
                    wait(pe, pT_ready, r.n)
                    for t in range(2):
                        i = pe.transpose(ps_p[:, t * P:(t + 1) * P], probs[:, t, :], ident[:, :])
                    i.then_inc(pT_done, 1)
                if at_stage(k, 1):
                    pe.wait_ge(xn_ready, (n + 1).n)
                    wait(pe, xnT_ready, n.n)
                    transposes(ps_x, lambda t, c: xn[:, n.slot(2), t, c]).then_inc(xT_done, 1)
                if at_stage(k, 2):
                    pe.wait_ge(pT_ready, (r + 1).n)
                    wait(pe, x2_done, r.n)
                    for t in range(2):
                        i = pe.matmul(ps_r[:, t, :], probsT[:, t, :], ctx_sb[:, r.slot(2), t, :], start=True, stop=True)
                    i.then_inc(readout_done, 1)
                if at_stage(k, 1):
                    pe.wait_ge(xnT_ready, (n + 1).n)
                    pe.wait_ge(ctxT_ready, (n + 1).n)
                    wait(pe, exp_done, n.n)
                    if k.i is None and k.c == 1:
                        pe.wait_ge(bias_ready, 1)
                    for t in range(2):
                        o = ps_s[:, t * P:(t + 1) * P]
                        for kd in range(KD):
                            pe.matmul(o, xnT[:, kd, t * P:(t + 1) * P], ctxT[:, kd, t * P:(t + 1) * P],
                                      start=(kd == 0), stop=False)
                        i = pe.matmul(o, batch_of[:, :], bias[:, bass.ds(n.n * 2 + t, 1), :].rearrange("b t m -> b (t m)"),
                                      start=False, stop=True)
                    i.then_inc(scores_ready, 1)
                if k.i is None and k.c == 1:
                    pe.wait_ge(any_ready, 1)
                    pe.matmul(ps_b[:, 0:T], batch_of[:, :], any2[:, :], start=True, stop=True).then_inc(valid_ready, 1)

            pairs(pe, turn)

            pe.wait_ge(onehot_ready, 2)
            oh = onehot[:, :, :].rearrange("p e t -> p (e t)")
            pe.matmul(ps_x[:, 0, 0:E * T], ones_b[:, :], oh, start=True, stop=True)
            pe.matmul(ps_c[:, 0, 0:E * T], tri_b[:, :], oh, start=True, stop=True).then_inc(counts_done, 1)
            pe.wait_ge(aval_ready, 1)
            for t in range(T):
                pe.wait_ge(hot_ready, GROUPS * t // T + 1)
                i = pe.matmul(ps_s[:, 0:SL], b_hot[:, t, :], a_val[:, t, :], start=(t == 0), stop=(t == T - 1))
            i.then_inc(slots_done, 1)

            def x_t(j):
                pe.wait_ge(fx_ready, (j + 1).n)
                wait(pe, xlo_ready, j.n)
                for k in range(KD):
                    i = pe.transpose(pf_x[:, k, :], fx[:, k * P:(k + 1) * P], ident[:, :])
                i.then_inc(fxT_done, 1)

            def half(bank, e, m, ready):
                for k in range(KD):
                    at = bass.ds(e * (2 * WM) + (m * WM + k * I), I)
                    pe.matmul(bank[:, :], fxT_hi[:, k, :], w_hi[:, at], start=(k == 0), stop=False)
                    pe.matmul(bank[:, :], fxT_hi[:, k, :], w_lo[:, at], start=False, stop=False)
                    i = pe.matmul(bank[:, :], fxT_lo[:, k, :], w_hi[:, at], start=False, stop=(k == KD - 1))
                i.then_inc(ready, 1)

            def expert(j):
                return pe.value_load(tile_expert[0:1, bass.ds(j.n, 1)], min_val=0, max_val=E - 1)

            def down(j):
                e = expert(j)
                apart(pe, (hTlo_ready, (j + 1).n), (y_ready, j.n))
                for k in range(KI):
                    at = bass.ds(e * WDN + k * D, D)
                    pe.matmul(pf_y[:, 0:D], hT_hi[:, k, :], d_hi[:, at], start=(k == 0), stop=False)
                    pe.matmul(pf_y[:, 0:D], hT_hi[:, k, :], d_lo[:, at], start=False, stop=False)
                    i = pe.matmul(pf_y[:, 0:D], hT_lo[:, k, :], d_hi[:, at], start=False, stop=(k == KI - 1))
                i.then_inc(down_done, 1)

            for t in range(WARM):
                pe.matmul(pf_g[:, :], b_hot[:, 0, :], b_hot[:, 0:4, :].rearrange("p t m -> p (t m)"), start=True, stop=True)
            pe.wait_ge(expert_ready, 1)
            x_t(At(None, 0, 0))

            def tile(j):
                e = expert(j)
                apart(pe, (xlo_ready, (j + 1).n))
                wait(pe, silu_done, j.n)
                half(pf_g, e, 0, g_done)
                wait(pe, h_ready, j.n)
                half(pf_u, e, 1, u_done)
                if not last(j):
                    x_t(j + 1)
                if j.i is not None or j.c > 0:
                    down(j - 1)
                pe.wait_ge(h_ready, (j + 1).n)
                wait(pe, hTlo_ready, j.n)
                for k in range(KI):
                    i = pe.transpose(pf_h[:, k, :], h[:, k * P:(k + 1) * P], ident[:, :])
                i.then_inc(hT_done, 1)
                if j.i is None and j.c == 0:
                    pe.wait_ge(d_lo_ready, 4)
                    pe.wait_ge(d_lo_ready_dve, 4)

            tiles(pe, tile, down, lambda: read_used(pe))


_INS = ["x", "ctx_2048", "mask_BxS2_bk0", "g_xattn", "g_ffn", "L0_ffn_router_w", "L0_ffn_gate_w",
        "L0_ffn_up_w", "L0_ffn_down_w"]


def kernel(**inputs):
    import numpy as np
    import concourse.bacc as bacc
    from concourse.bass_utils import run_bass_kernel_spmd

    nc = bacc.Bacc("TRN2", target_bir_lowering=False, num_devices=1)
    arrays, args = {}, []
    for name in _INS:
        v = np.ascontiguousarray(inputs[name])
        arrays[f"in_{name}"] = v
        args.append(nc.dram_tensor(f"in_{name}", v.shape, mybir.dt.from_np(v.dtype), kind="ExternalInput").ap())
    out = nc.dram_tensor("out", inputs["x"].shape, F32, kind="ExternalOutput").ap()
    gated_block(nc, *args, out)
    r = run_bass_kernel_spmd(nc, [arrays], core_ids=[0])
    return r.results[0]["out"]
```
